# Optimizing a Trainium2 kernel written in Bass

```python
import numpy as np
import jax
import jax.numpy as jnp

def _softmax(x, axis=-1):
    return jax.nn.softmax(x, axis=axis)

def _gelu(x):
    return jax.nn.gelu(x, approximate=True)

def _silu(x):
    return jax.nn.silu(x)

def _sigmoid(x):
    return jax.nn.sigmoid(x)

def _layernorm(x, axis=-1, eps=1e-05):
    m = jnp.mean(x, axis=axis, keepdims=True)
    v = jnp.var(x, axis=axis, keepdims=True)
    return (x - m) / jnp.sqrt(v + eps)

def _scatter_add(tgt, idx, src, axis=0):
    return tgt.at[idx].add(src)

def _segment_sum(src, seg, n):
    return jax.ops.segment_sum(src, seg, n)
kernel_name = 'mk_vit_tower_postln_d2_tok_img512_r4_af892c'

def setup_inputs(seed: int=0):
    np.random.seed(seed)
    _w = jnp.asarray

    def _rec_inputs():
        import jax
        import jax.numpy as jnp
        _rk = jax.random.key(seed)
        x = -0.000190493 + 0.999948 * jax.random.normal(jax.random.fold_in(_rk, 1), (128, 2, 104, 104), jnp.float32)
        return x
    x = _rec_inputs()

    def _L0_tok_setup():
        import jax, jax.numpy as jnp
        import numpy as np
        HP = 4
        PATCH = 8
        EPS = 1e-07

        def _shifts(x):
            h, w = (x.shape[2], x.shape[3])
            pad2 = ((0, 0), (0, 0))
            left_up = jnp.pad(x[:, :, HP:, :w - HP], pad2 + ((0, HP), (HP, 0)))
            right_up = jnp.pad(x[:, :, HP:, HP:], pad2 + ((0, HP), (0, HP)))
            left_down = jnp.pad(x[:, :, :h - HP, :w - HP], pad2 + ((HP, 0), (HP, 0)))
            right_down = jnp.pad(x[:, :, :h - HP, HP:], pad2 + ((HP, 0), (0, HP)))
            return (left_up, right_up, left_down, right_down)
        key = jax.random.key(seed)
        k1, k2, k3, k4 = jax.random.split(key, 4)
        B, C, S = (128, 2, 104)
        embed_dim = 128
        x = jax.random.normal(k1, (B, C, S, S), dtype=jnp.float32)
        gamma = 1.0 + 0.05 * jax.random.normal(k2, (10, S, S), dtype=jnp.float32)
        beta = 0.05 * jax.random.normal(k3, (10, S, S), dtype=jnp.float32)
        W = 0.02 * jax.random.normal(k4, (embed_dim, 10, PATCH, PATCH), dtype=jnp.float32)
        b = jnp.zeros((embed_dim,), dtype=jnp.float32)
        return {'x': x, 'gamma': gamma, 'beta': beta, 'W': W, 'b': b}
    _L0_tok_all = _L0_tok_setup()
    _L0_tok_in = {k: v for k, v in _L0_tok_all.items() if k in ('gamma', 'beta', 'W', 'b')}
    del _L0_tok_all

    def _L0_attn_setup():
        import jax, jax.numpy as jnp
        import numpy as np
        D_MODEL = 128
        D_STATE = 16
        D_CONV = 4
        D_INNER = 256
        HEADS = 8
        D_K = D_MODEL // HEADS
        EPS = 1e-05

        def layer_norm(x, g, b):
            mu = jnp.mean(x, axis=-1, keepdims=True)
            var = jnp.var(x, axis=-1, keepdims=True)
            return (x - mu) / jnp.sqrt(var + EPS) * g + b

        def silu(x):
            return x * jax.nn.sigmoid(x)

        def selective_scan(u, delta, A, B, C, Dp):

            def step(h, inp):
                u_i, d_i, B_i, C_i = inp
                dA = jnp.exp(d_i[:, None, :] * A[None, :, None])
                h = h * dA + d_i[:, None, :] * B_i[:, :, None] * u_i[:, None, :]
                y_i = jnp.sum(h * C_i[:, :, None], axis=1)
                return (h, y_i)
            b = u.shape[0]
            h0 = jnp.zeros((b, A.shape[0], u.shape[-1]), u.dtype)
            xs = (u.transpose(1, 0, 2), delta.transpose(1, 0, 2), B.transpose(1, 0, 2), C.transpose(1, 0, 2))
            _, ys = jax.lax.scan(step, h0, xs)
            y = ys.transpose(1, 0, 2)
            return y + u * Dp

        def mamba(x, in_proj_w, conv_w, conv_b, x_proj_w, dt_proj_w, dt_proj_b, A_log, Dp, out_proj_w):
            L = x.shape[1]
            xr = x @ in_proj_w
            xm, res = jnp.split(xr, 2, axis=-1)
            xp = jnp.pad(xm, ((0, 0), (D_CONV - 1, 0), (0, 0)))
            xc = sum((conv_w[:, k] * xp[:, k:k + L, :] for k in range(D_CONV))) + conv_b
            xc = silu(xc)
            BC = xc @ x_proj_w
            B, C = jnp.split(BC, 2, axis=-1)
            delta = jax.nn.softplus(xc @ dt_proj_w + dt_proj_b)
            A = -jnp.exp(A_log)
            y = selective_scan(xc, delta, A, B, C, Dp)
            y = y * silu(res)
            return y @ out_proj_w

        def attention(q_in, wq_w, wq_b, wk_w, wk_b, wv_w, wv_b, wo_w, wo_b, ln_g, ln_b):
            b, S, _ = q_in.shape
            Q = (q_in @ wq_w + wq_b).reshape(b, S, HEADS, D_K)
            K = (q_in @ wk_w + wk_b).reshape(b, S, HEADS, D_K)
            V = (q_in @ wv_w + wv_b).reshape(b, S, HEADS, D_K)
            scores = jnp.einsum('bqhd,bkhd->bhqk', Q, K) / np.sqrt(D_K).astype(np.float32)
            w = jax.nn.softmax(scores, axis=-1)
            out = jnp.einsum('bhqk,bkhd->bqhd', w, V).reshape(b, S, D_MODEL)
            out = out @ wo_w + wo_b
            return (layer_norm(out + q_in, ln_g, ln_b), w)

        def _reference_tuple_inner(x, in_proj_w, conv_w, conv_b, x_proj_w, dt_proj_w, dt_proj_b, A_log, D, out_proj_w, wq_w, wq_b, wk_w, wk_b, wv_w, wv_b, wo_w, wo_b, attn_ln_g, attn_ln_b, ffn_w1, ffn_b1, ffn_w2, ffn_b2, norm1_g, norm1_b, norm2_g, norm2_b, norm3_g, norm3_b, gate_w, gate_b):
            mamba_out = mamba(layer_norm(x, norm1_g, norm1_b), in_proj_w, conv_w, conv_b, x_proj_w, dt_proj_w, dt_proj_b, A_log, D, out_proj_w)
            x = x + mamba_out
            xn = layer_norm(x, norm2_g, norm2_b)
            attn_out, attn_w = attention(xn, wq_w, wq_b, wk_w, wk_b, wv_w, wv_b, wo_w, wo_b, attn_ln_g, attn_ln_b)
            x = x + attn_out
            combined = jnp.concatenate([mamba_out, attn_out], axis=-1)
            g = jax.nn.sigmoid(combined @ gate_w + gate_b)
            fused = g * mamba_out + (1.0 - g) * attn_out
            x = x + fused
            xn3 = layer_norm(x, norm3_g, norm3_b)
            ffn = jax.nn.gelu(xn3 @ ffn_w1 + ffn_b1) @ ffn_w2 + ffn_b2
            x = x + ffn
            return (x, attn_w)
        key = jax.random.key(seed)
        ks = jax.random.split(key, 20)
        s = 0.02

        def n(k, shape):
            return jax.random.normal(k, shape, jnp.float32) * s
        inp = {'x': jax.random.normal(ks[0], (8, 256, D_MODEL), jnp.float32), 'in_proj_w': n(ks[1], (D_MODEL, 2 * D_INNER)), 'conv_w': n(ks[2], (D_INNER, D_CONV)), 'conv_b': jnp.zeros((D_INNER,), jnp.float32), 'x_proj_w': n(ks[3], (D_INNER, 2 * D_STATE)), 'dt_proj_w': n(ks[4], (D_INNER, D_INNER)), 'dt_proj_b': jnp.zeros((D_INNER,), jnp.float32), 'A_log': jnp.log(jnp.arange(1, D_STATE + 1, dtype=jnp.float32)), 'D': jnp.ones((D_INNER,), jnp.float32), 'out_proj_w': n(ks[5], (D_INNER, D_MODEL)), 'wq_w': n(ks[6], (D_MODEL, D_MODEL)), 'wq_b': jnp.zeros((D_MODEL,), jnp.float32), 'wk_w': n(ks[7], (D_MODEL, D_MODEL)), 'wk_b': jnp.zeros((D_MODEL,), jnp.float32), 'wv_w': n(ks[8], (D_MODEL, D_MODEL)), 'wv_b': jnp.zeros((D_MODEL,), jnp.float32), 'wo_w': n(ks[9], (D_MODEL, D_MODEL)), 'wo_b': jnp.zeros((D_MODEL,), jnp.float32), 'attn_ln_g': jnp.ones((D_MODEL,), jnp.float32), 'attn_ln_b': jnp.zeros((D_MODEL,), jnp.float32), 'ffn_w1': n(ks[10], (D_MODEL, 4 * D_MODEL)), 'ffn_b1': jnp.zeros((4 * D_MODEL,), jnp.float32), 'ffn_w2': n(ks[11], (4 * D_MODEL, D_MODEL)), 'ffn_b2': jnp.zeros((D_MODEL,), jnp.float32), 'norm1_g': jnp.ones((D_MODEL,), jnp.float32), 'norm1_b': jnp.zeros((D_MODEL,), jnp.float32), 'norm2_g': jnp.ones((D_MODEL,), jnp.float32), 'norm2_b': jnp.zeros((D_MODEL,), jnp.float32), 'norm3_g': jnp.ones((D_MODEL,), jnp.float32), 'norm3_b': jnp.zeros((D_MODEL,), jnp.float32), 'gate_w': n(ks[12], (2 * D_MODEL, D_MODEL)), 'gate_b': jnp.zeros((D_MODEL,), jnp.float32)}
        return inp
    _L0_attn_all = _L0_attn_setup()
    _L0_attn_in = {k: v for k, v in _L0_attn_all.items() if k in ('in_proj_w', 'conv_w', 'conv_b', 'x_proj_w', 'dt_proj_w', 'dt_proj_b', 'A_log', 'D', 'out_proj_w', 'wq_w', 'wq_b', 'wk_w', 'wk_b', 'wv_w', 'wv_b', 'wo_w', 'wo_b', 'attn_ln_g', 'attn_ln_b', 'ffn_w1', 'ffn_b1', 'ffn_w2', 'ffn_b2', 'norm1_g', 'norm1_b', 'norm2_g', 'norm2_b', 'norm3_g', 'norm3_b', 'gate_w', 'gate_b')}
    del _L0_attn_all

    def _L0_ffn_setup():
        import jax, jax.numpy as jnp
        import numpy as np
        from jax import lax
        N, M, DIM, HEADS, TOPK = (4, 512, 128, 8, 16)

        def _split_heads(t, h):
            n, m, c = t.shape
            return t.reshape(n, m, h, c // h).transpose(0, 2, 1, 3).reshape(n * h, m, c // h)
        key = jax.random.key(seed)
        ks = jax.random.split(key, 7)
        f = lambda k, s, sc=1.0: jax.random.normal(k, s, dtype=jnp.float32) * sc
        return {'x': f(ks[0], (N, M, DIM)), 'pos_w': f(ks[1], (DIM, 1, 3), 0.1), 'pos_b': f(ks[2], (DIM,), 0.02), 'qkv_w': f(ks[3], (3 * DIM, DIM), 0.02), 'qkv_b': f(ks[4], (3 * DIM,), 0.02), 'wo_w': f(ks[5], (DIM, DIM), 0.02), 'wo_b': f(ks[6], (DIM,), 0.02)}
    _L0_ffn_all = _L0_ffn_setup()
    _L0_ffn_in = {k: v for k, v in _L0_ffn_all.items() if k in ('pos_w', 'pos_b', 'qkv_w', 'qkv_b', 'wo_w', 'wo_b')}
    del _L0_ffn_all

    def _L1_attn_setup():
        import jax, jax.numpy as jnp
        import numpy as np
        B, S, D = (8, 512, 128)
        HEADS = 8
        DEPTH = D // HEADS
        SCALE = DEPTH ** (-0.5)
        LN_EPS = 0.001
        key = jax.random.key(seed)
        ks = jax.random.split(key, 9)

        def w(k, shape, scale=0.02):
            return jax.random.normal(k, shape, dtype=jnp.float32) * scale
        return {'x': jax.random.normal(ks[0], (B, S, D), dtype=jnp.float32), 'Wq': w(ks[1], (D, D)), 'bq': jnp.zeros((D,), jnp.float32), 'Wk': w(ks[2], (D, D)), 'bk': jnp.zeros((D,), jnp.float32), 'Wv': w(ks[3], (D, D)), 'bv': jnp.zeros((D,), jnp.float32), 'Wo': w(ks[4], (D, D)), 'bo': jnp.zeros((D,), jnp.float32), 'gamma': jnp.ones((D,), jnp.float32), 'beta': jnp.zeros((D,), jnp.float32)}
    _L1_attn_all = _L1_attn_setup()
    _L1_attn_in = {k: v for k, v in _L1_attn_all.items() if k in ('Wq', 'bq', 'Wk', 'bk', 'Wv', 'bv', 'Wo', 'bo', 'gamma', 'beta')}
    del _L1_attn_all

    def _L1_ffn_setup():
        import jax, jax.numpy as jnp
        import numpy as np
        D, H, E, B, S = (128, 512, 16, 8, 2048)
        MAX_GROUP_SIZE = 1024
        MIN_CAPACITY = 8
        CAPACITY_FACTOR = 1.0

        def _group_dims(num_tokens, num_experts):
            num_groups = -(-num_tokens // MAX_GROUP_SIZE)
            while num_tokens % num_groups != 0 or num_groups % num_experts != 0:
                num_groups += 1
            return (num_tokens // num_groups, num_groups)
        key = jax.random.key(seed)
        ks = jax.random.split(key, 6)
        s = 0.02
        return {'x': jax.random.normal(ks[0], (B, S, D), jnp.float32), 'gate_w': jax.random.normal(ks[1], (D, E), jnp.float32) * s, 'w1': jax.random.normal(ks[2], (E, D, H), jnp.float32) * s, 'b1': jnp.zeros((E, H), jnp.float32), 'w2': jax.random.normal(ks[3], (E, H, D), jnp.float32) * s, 'b2': jnp.zeros((E, D), jnp.float32), 'sw1': jax.random.normal(ks[4], (D, H), jnp.float32) * s, 'sb1': jnp.zeros((H,), jnp.float32), 'sw2': jax.random.normal(ks[5], (H, D), jnp.float32) * s, 'sb2': jnp.zeros((D,), jnp.float32)}
    _L1_ffn_all = _L1_ffn_setup()
    _L1_ffn_in = {k: v for k, v in _L1_ffn_all.items() if k in ('gate_w', 'w1', 'b1', 'w2', 'b2', 'sw1', 'sb1', 'sw2', 'sb2')}
    del _L1_ffn_all
    return {'x': x, 'L0_tok_gamma': _L0_tok_in['gamma'], 'L0_tok_beta': _L0_tok_in['beta'], 'L0_tok_W': _L0_tok_in['W'], 'L0_tok_b': _L0_tok_in['b'], 'L0_attn_in_proj_w': _L0_attn_in['in_proj_w'], 'L0_attn_conv_w': _L0_attn_in['conv_w'], 'L0_attn_conv_b': _L0_attn_in['conv_b'], 'L0_attn_x_proj_w': _L0_attn_in['x_proj_w'], 'L0_attn_dt_proj_w': _L0_attn_in['dt_proj_w'], 'L0_attn_dt_proj_b': _L0_attn_in['dt_proj_b'], 'L0_attn_A_log': _L0_attn_in['A_log'], 'L0_attn_D': _L0_attn_in['D'], 'L0_attn_out_proj_w': _L0_attn_in['out_proj_w'], 'L0_attn_wq_w': _L0_attn_in['wq_w'], 'L0_attn_wq_b': _L0_attn_in['wq_b'], 'L0_attn_wk_w': _L0_attn_in['wk_w'], 'L0_attn_wk_b': _L0_attn_in['wk_b'], 'L0_attn_wv_w': _L0_attn_in['wv_w'], 'L0_attn_wv_b': _L0_attn_in['wv_b'], 'L0_attn_wo_w': _L0_attn_in['wo_w'], 'L0_attn_wo_b': _L0_attn_in['wo_b'], 'L0_attn_attn_ln_g': _L0_attn_in['attn_ln_g'], 'L0_attn_attn_ln_b': _L0_attn_in['attn_ln_b'], 'L0_attn_ffn_w1': _L0_attn_in['ffn_w1'], 'L0_attn_ffn_b1': _L0_attn_in['ffn_b1'], 'L0_attn_ffn_w2': _L0_attn_in['ffn_w2'], 'L0_attn_ffn_b2': _L0_attn_in['ffn_b2'], 'L0_attn_norm1_g': _L0_attn_in['norm1_g'], 'L0_attn_norm1_b': _L0_attn_in['norm1_b'], 'L0_attn_norm2_g': _L0_attn_in['norm2_g'], 'L0_attn_norm2_b': _L0_attn_in['norm2_b'], 'L0_attn_norm3_g': _L0_attn_in['norm3_g'], 'L0_attn_norm3_b': _L0_attn_in['norm3_b'], 'L0_attn_gate_w': _L0_attn_in['gate_w'], 'L0_attn_gate_b': _L0_attn_in['gate_b'], 'L0_ffn_pos_w': _L0_ffn_in['pos_w'], 'L0_ffn_pos_b': _L0_ffn_in['pos_b'], 'L0_ffn_qkv_w': _L0_ffn_in['qkv_w'], 'L0_ffn_qkv_b': _L0_ffn_in['qkv_b'], 'L0_ffn_wo_w': _L0_ffn_in['wo_w'], 'L0_ffn_wo_b': _L0_ffn_in['wo_b'], 'L1_attn_Wq': _L1_attn_in['Wq'], 'L1_attn_bq': _L1_attn_in['bq'], 'L1_attn_Wk': _L1_attn_in['Wk'], 'L1_attn_bk': _L1_attn_in['bk'], 'L1_attn_Wv': _L1_attn_in['Wv'], 'L1_attn_bv': _L1_attn_in['bv'], 'L1_attn_Wo': _L1_attn_in['Wo'], 'L1_attn_bo': _L1_attn_in['bo'], 'L1_attn_gamma': _L1_attn_in['gamma'], 'L1_attn_beta': _L1_attn_in['beta'], 'L1_ffn_gate_w': _L1_ffn_in['gate_w'], 'L1_ffn_w1': _L1_ffn_in['w1'], 'L1_ffn_b1': _L1_ffn_in['b1'], 'L1_ffn_w2': _L1_ffn_in['w2'], 'L1_ffn_b2': _L1_ffn_in['b2'], 'L1_ffn_sw1': _L1_ffn_in['sw1'], 'L1_ffn_sb1': _L1_ffn_in['sb1'], 'L1_ffn_sw2': _L1_ffn_in['sw2'], 'L1_ffn_sb2': _L1_ffn_in['sb2']}

def reference(x, L0_tok_gamma, L0_tok_beta, L0_tok_W, L0_tok_b, L0_attn_in_proj_w, L0_attn_conv_w, L0_attn_conv_b, L0_attn_x_proj_w, L0_attn_dt_proj_w, L0_attn_dt_proj_b, L0_attn_A_log, L0_attn_D, L0_attn_out_proj_w, L0_attn_wq_w, L0_attn_wq_b, L0_attn_wk_w, L0_attn_wk_b, L0_attn_wv_w, L0_attn_wv_b, L0_attn_wo_w, L0_attn_wo_b, L0_attn_attn_ln_g, L0_attn_attn_ln_b, L0_attn_ffn_w1, L0_attn_ffn_b1, L0_attn_ffn_w2, L0_attn_ffn_b2, L0_attn_norm1_g, L0_attn_norm1_b, L0_attn_norm2_g, L0_attn_norm2_b, L0_attn_norm3_g, L0_attn_norm3_b, L0_attn_gate_w, L0_attn_gate_b, L0_ffn_pos_w, L0_ffn_pos_b, L0_ffn_qkv_w, L0_ffn_qkv_b, L0_ffn_wo_w, L0_ffn_wo_b, L1_attn_Wq, L1_attn_bq, L1_attn_Wk, L1_attn_bk, L1_attn_Wv, L1_attn_bv, L1_attn_Wo, L1_attn_bo, L1_attn_gamma, L1_attn_beta, L1_ffn_gate_w, L1_ffn_w1, L1_ffn_b1, L1_ffn_w2, L1_ffn_b2, L1_ffn_sw1, L1_ffn_sb1, L1_ffn_sw2, L1_ffn_sb2):
    import jax
    import jax.numpy as jnp

    def _L0_tok_ref(x, gamma, beta, W, b):
        import jax, jax.numpy as jnp
        import numpy as np
        HP = 4
        PATCH = 8
        EPS = 1e-07

        def _shifts(x):
            h, w = (x.shape[2], x.shape[3])
            pad2 = ((0, 0), (0, 0))
            left_up = jnp.pad(x[:, :, HP:, :w - HP], pad2 + ((0, HP), (HP, 0)))
            right_up = jnp.pad(x[:, :, HP:, HP:], pad2 + ((0, HP), (0, HP)))
            left_down = jnp.pad(x[:, :, :h - HP, :w - HP], pad2 + ((HP, 0), (HP, 0)))
            right_down = jnp.pad(x[:, :, :h - HP, HP:], pad2 + ((HP, 0), (0, HP)))
            return (left_up, right_up, left_down, right_down)
        lu, ru, ld, rd = _shifts(x)
        concat = jnp.concatenate((x, lu, ru, ld, rd), axis=1)
        mean = jnp.mean(concat, axis=(1, 2, 3), keepdims=True)
        var = jnp.var(concat, axis=(1, 2, 3), keepdims=True)
        normed = (concat - mean) * jax.lax.rsqrt(var + EPS)
        normed = normed * gamma[None] + beta[None]
        y = jax.lax.conv_general_dilated(normed, W, window_strides=(PATCH, PATCH), padding='VALID', dimension_numbers=('NCHW', 'OIHW', 'NCHW'))
        y = y + b[None, :, None, None]
        B, E = (y.shape[0], y.shape[1])
        y = y.reshape(B, E, -1).transpose(0, 2, 1)
        return y

    def _L0_attn_ref(x, in_proj_w, conv_w, conv_b, x_proj_w, dt_proj_w, dt_proj_b, A_log, D, out_proj_w, wq_w, wq_b, wk_w, wk_b, wv_w, wv_b, wo_w, wo_b, attn_ln_g, attn_ln_b, ffn_w1, ffn_b1, ffn_w2, ffn_b2, norm1_g, norm1_b, norm2_g, norm2_b, norm3_g, norm3_b, gate_w, gate_b):
        import jax, jax.numpy as jnp
        import numpy as np
        D_MODEL = 128
        D_STATE = 16
        D_CONV = 4
        D_INNER = 256
        HEADS = 8
        D_K = D_MODEL // HEADS
        EPS = 1e-05

        def layer_norm(x, g, b):
            mu = jnp.mean(x, axis=-1, keepdims=True)
            var = jnp.var(x, axis=-1, keepdims=True)
            return (x - mu) / jnp.sqrt(var + EPS) * g + b

        def silu(x):
            return x * jax.nn.sigmoid(x)

        def selective_scan(u, delta, A, B, C, Dp):

            def step(h, inp):
                u_i, d_i, B_i, C_i = inp
                dA = jnp.exp(d_i[:, None, :] * A[None, :, None])
                h = h * dA + d_i[:, None, :] * B_i[:, :, None] * u_i[:, None, :]
                y_i = jnp.sum(h * C_i[:, :, None], axis=1)
                return (h, y_i)
            b = u.shape[0]
            h0 = jnp.zeros((b, A.shape[0], u.shape[-1]), u.dtype)
            xs = (u.transpose(1, 0, 2), delta.transpose(1, 0, 2), B.transpose(1, 0, 2), C.transpose(1, 0, 2))
            _, ys = jax.lax.scan(step, h0, xs)
            y = ys.transpose(1, 0, 2)
            return y + u * Dp

        def mamba(x, in_proj_w, conv_w, conv_b, x_proj_w, dt_proj_w, dt_proj_b, A_log, Dp, out_proj_w):
            L = x.shape[1]
            xr = x @ in_proj_w
            xm, res = jnp.split(xr, 2, axis=-1)
            xp = jnp.pad(xm, ((0, 0), (D_CONV - 1, 0), (0, 0)))
            xc = sum((conv_w[:, k] * xp[:, k:k + L, :] for k in range(D_CONV))) + conv_b
            xc = silu(xc)
            BC = xc @ x_proj_w
            B, C = jnp.split(BC, 2, axis=-1)
            delta = jax.nn.softplus(xc @ dt_proj_w + dt_proj_b)
            A = -jnp.exp(A_log)
            y = selective_scan(xc, delta, A, B, C, Dp)
            y = y * silu(res)
            return y @ out_proj_w

        def attention(q_in, wq_w, wq_b, wk_w, wk_b, wv_w, wv_b, wo_w, wo_b, ln_g, ln_b):
            b, S, _ = q_in.shape
            Q = (q_in @ wq_w + wq_b).reshape(b, S, HEADS, D_K)
            K = (q_in @ wk_w + wk_b).reshape(b, S, HEADS, D_K)
            V = (q_in @ wv_w + wv_b).reshape(b, S, HEADS, D_K)
            scores = jnp.einsum('bqhd,bkhd->bhqk', Q, K) / np.sqrt(D_K).astype(np.float32)
            w = jax.nn.softmax(scores, axis=-1)
            out = jnp.einsum('bhqk,bkhd->bqhd', w, V).reshape(b, S, D_MODEL)
            out = out @ wo_w + wo_b
            return (layer_norm(out + q_in, ln_g, ln_b), w)

        def _reference_tuple_inner(x, in_proj_w, conv_w, conv_b, x_proj_w, dt_proj_w, dt_proj_b, A_log, D, out_proj_w, wq_w, wq_b, wk_w, wk_b, wv_w, wv_b, wo_w, wo_b, attn_ln_g, attn_ln_b, ffn_w1, ffn_b1, ffn_w2, ffn_b2, norm1_g, norm1_b, norm2_g, norm2_b, norm3_g, norm3_b, gate_w, gate_b):
            mamba_out = mamba(layer_norm(x, norm1_g, norm1_b), in_proj_w, conv_w, conv_b, x_proj_w, dt_proj_w, dt_proj_b, A_log, D, out_proj_w)
            x = x + mamba_out
            xn = layer_norm(x, norm2_g, norm2_b)
            attn_out, attn_w = attention(xn, wq_w, wq_b, wk_w, wk_b, wv_w, wv_b, wo_w, wo_b, attn_ln_g, attn_ln_b)
            x = x + attn_out
            combined = jnp.concatenate([mamba_out, attn_out], axis=-1)
            g = jax.nn.sigmoid(combined @ gate_w + gate_b)
            fused = g * mamba_out + (1.0 - g) * attn_out
            x = x + fused
            xn3 = layer_norm(x, norm3_g, norm3_b)
            ffn = jax.nn.gelu(xn3 @ ffn_w1 + ffn_b1) @ ffn_w2 + ffn_b2
            x = x + ffn
            return (x, attn_w)
        return _reference_tuple_inner(x, in_proj_w, conv_w, conv_b, x_proj_w, dt_proj_w, dt_proj_b, A_log, D, out_proj_w, wq_w, wq_b, wk_w, wk_b, wv_w, wv_b, wo_w, wo_b, attn_ln_g, attn_ln_b, ffn_w1, ffn_b1, ffn_w2, ffn_b2, norm1_g, norm1_b, norm2_g, norm2_b, norm3_g, norm3_b, gate_w, gate_b)[0]

    def _L0_ffn_ref(x, pos_w, pos_b, qkv_w, qkv_b, wo_w, wo_b):
        import jax, jax.numpy as jnp
        import numpy as np
        from jax import lax
        N, M, DIM, HEADS, TOPK = (4, 512, 128, 8, 16)

        def _split_heads(t, h):
            n, m, c = t.shape
            return t.reshape(n, m, h, c // h).transpose(0, 2, 1, 3).reshape(n * h, m, c // h)
        n, m, c = x.shape
        h = HEADS
        scale = c ** (-0.5)
        pos = lax.conv_general_dilated(x.transpose(0, 2, 1), pos_w, window_strides=(1,), padding=[(1, 1)], feature_group_count=c, dimension_numbers=('NCH', 'OIH', 'NCH'))
        x = x + (pos + pos_b[None, :, None]).transpose(0, 2, 1)
        qkv = x @ qkv_w.T + qkv_b
        q, k, v = jnp.split(qkv, [c, 2 * c], axis=-1)
        q = _split_heads(q, h)
        k = _split_heads(k, h)
        v = _split_heads(v, h)
        qd = lax.stop_gradient(q)
        kd = lax.stop_gradient(k)
        logits = jnp.einsum('bmd,bpd->bmp', qd * scale, kd)
        _, idx = lax.top_k(logits, TOPK)
        gather = jax.vmap(lambda t, i: t[i])
        k_sel = gather(k, idx)
        v_sel = gather(v, idx)
        attn = jax.nn.softmax(jnp.einsum('bmd,bmkd->bmk', q * scale, k_sel), axis=-1)
        out = jnp.einsum('bmk,bmkd->bmd', attn, v_sel)
        d = c // h
        out = out.reshape(n, h, m, d).transpose(0, 2, 1, 3).reshape(n, m, c)
        return out @ wo_w.T + wo_b

    def _L1_attn_ref(x, Wq, bq, Wk, bk, Wv, bv, Wo, bo, gamma, beta):
        import jax, jax.numpy as jnp
        import numpy as np
        B, S, D = (8, 512, 128)
        HEADS = 8
        DEPTH = D // HEADS
        SCALE = DEPTH ** (-0.5)
        LN_EPS = 0.001
        q = jax.nn.relu(x @ Wq + bq) * SCALE
        k = jax.nn.relu(x @ Wk + bk)
        v = jax.nn.relu(x @ Wv + bv)
        scores = jnp.einsum('bsd,btd->bst', q, k)
        attn = jax.nn.softmax(scores, axis=-1)
        ctx = jnp.einsum('bst,btd->bsd', attn, v)
        out = jax.nn.relu(ctx @ Wo + bo)
        mu = jnp.mean(out, axis=-1, keepdims=True)
        var = jnp.var(out, axis=-1, keepdims=True)
        return (out - mu) * jax.lax.rsqrt(var + LN_EPS) * gamma + beta

    def _L1_ffn_ref(x, gate_w, w1, b1, w2, b2, sw1, sb1, sw2, sb2):
        import jax, jax.numpy as jnp
        import numpy as np
        D, H, E, B, S = (128, 512, 16, 8, 2048)
        MAX_GROUP_SIZE = 1024
        MIN_CAPACITY = 8
        CAPACITY_FACTOR = 1.0

        def _group_dims(num_tokens, num_experts):
            num_groups = -(-num_tokens // MAX_GROUP_SIZE)
            while num_tokens % num_groups != 0 or num_groups % num_experts != 0:
                num_groups += 1
            return (num_tokens // num_groups, num_groups)
        Bn, Sn, Dn = x.shape
        En = gate_w.shape[1]
        T = Bn * Sn
        group_size, num_groups = _group_dims(T, En)
        cap = max(int(round(CAPACITY_FACTOR * group_size * num_groups / En)), MIN_CAPACITY)
        xg = x.reshape(num_groups, group_size, Dn)
        logits = jnp.einsum('gsd,de->gse', xg, gate_w)
        probs = jax.nn.softmax(logits, axis=-1)
        flat_probs = probs.transpose(2, 0, 1).reshape(En, T)
        scores, tok_idx = jax.lax.top_k(flat_probs, cap)
        xf = x.reshape(T, Dn)
        toks = xf[tok_idx]
        h = jax.nn.gelu(jnp.einsum('ecd,edh->ech', toks, w1) + b1[:, None, :])
        y = jnp.einsum('ech,ehd->ecd', h, w2) + b2[:, None, :]
        y = y * scores[..., None]
        routed = jnp.zeros_like(xf).at[tok_idx.reshape(-1)].add(y.reshape(-1, Dn))
        shared = jax.nn.gelu(xf @ sw1 + sb1) @ sw2 + sb2
        out = (routed + shared).reshape(Bn, Sn, Dn)
        return out
    h = _L0_tok_ref(x, L0_tok_gamma, L0_tok_beta, L0_tok_W, L0_tok_b)
    h = _layernorm(h + _L0_attn_ref(h, L0_attn_in_proj_w, L0_attn_conv_w, L0_attn_conv_b, L0_attn_x_proj_w, L0_attn_dt_proj_w, L0_attn_dt_proj_b, L0_attn_A_log, L0_attn_D, L0_attn_out_proj_w, L0_attn_wq_w, L0_attn_wq_b, L0_attn_wk_w, L0_attn_wk_b, L0_attn_wv_w, L0_attn_wv_b, L0_attn_wo_w, L0_attn_wo_b, L0_attn_attn_ln_g, L0_attn_attn_ln_b, L0_attn_ffn_w1, L0_attn_ffn_b1, L0_attn_ffn_w2, L0_attn_ffn_b2, L0_attn_norm1_g, L0_attn_norm1_b, L0_attn_norm2_g, L0_attn_norm2_b, L0_attn_norm3_g, L0_attn_norm3_b, L0_attn_gate_w, L0_attn_gate_b), axis=-1)
    h = _layernorm(h + _L0_ffn_ref(h, L0_ffn_pos_w, L0_ffn_pos_b, L0_ffn_qkv_w, L0_ffn_qkv_b, L0_ffn_wo_w, L0_ffn_wo_b), axis=-1)
    h = _layernorm(h + _L1_attn_ref(h, L1_attn_Wq, L1_attn_bq, L1_attn_Wk, L1_attn_bk, L1_attn_Wv, L1_attn_bv, L1_attn_Wo, L1_attn_bo, L1_attn_gamma, L1_attn_beta), axis=-1)
    h = _layernorm(h + _L1_ffn_ref(h, L1_ffn_gate_w, L1_ffn_w1, L1_ffn_b1, L1_ffn_w2, L1_ffn_b2, L1_ffn_sw1, L1_ffn_sb1, L1_ffn_sw2, L1_ffn_sb2), axis=-1)
    return h

_drawn_inputs = setup_inputs


def setup_inputs(seed=0):
    import zlib

    import numpy as np

    out = dict(_drawn_inputs(seed))
    spreads = {'L0_tok_b': (0.0, 0.1),
     'L0_attn_conv_b': (0.0, 0.8),
     'L0_attn_dt_proj_b': (0.0, 0.8),
     'L0_attn_D': (1.0, 0.6),
     'L0_attn_wq_b': (0.0, 0.8),
     'L0_attn_wk_b': (0.0, 0.8),
     'L0_attn_wv_b': (0.0, 0.725),
     'L0_attn_wo_b': (0.0, 0.1),
     'L0_attn_attn_ln_g': (1.0, 0.2),
     'L0_attn_attn_ln_b': (0.0, 0.1),
     'L0_attn_ffn_b1': (0.0, 0.8),
     'L0_attn_ffn_b2': (0.0, 0.1),
     'L0_attn_norm1_g': (1.0, 0.6),
     'L0_attn_norm1_b': (0.0, 0.8),
     'L0_attn_norm2_g': (1.0, 0.2),
     'L0_attn_norm2_b': (0.0, 0.1),
     'L0_attn_norm3_g': (1.0, 0.6),
     'L0_attn_norm3_b': (0.0, 0.8),
     'L0_attn_gate_b': (0.0, 0.8),
     'L1_attn_bq': (0.0, 0.8),
     'L1_attn_bk': (0.0, 0.8),
     'L1_attn_bv': (0.0, 0.1),
     'L1_attn_bo': (0.0, 0.1),
     'L1_attn_gamma': (1.0, 0.2),
     'L1_attn_beta': (0.0, 0.1),
     'L1_ffn_b1': (0.0, 0.8),
     'L1_ffn_b2': (0.0, 0.8),
     'L1_ffn_sb1': (0.0, 0.356),
     'L1_ffn_sb2': (0.0, 0.1)}
    factors = {'L0_attn_in_proj_w': 8.0,
     'L0_attn_conv_w': 8.0,
     'L0_attn_x_proj_w': 8.0,
     'L0_attn_dt_proj_w': 8.0,
     'L0_attn_A_log': 8.0,
     'L0_attn_out_proj_w': 8.0,
     'L0_attn_wq_w': 8.0,
     'L0_attn_wk_w': 8.0,
     'L0_attn_wv_w': 8.0,
     'L0_attn_wo_w': 5.312,
     'L0_attn_ffn_w1': 3.475,
     'L0_attn_ffn_w2': 3.095,
     'L0_attn_gate_w': 3.408,
     'L0_ffn_pos_w': 8.0,
     'L0_ffn_pos_b': 8.0,
     'L0_ffn_qkv_w': 3.966,
     'L0_ffn_qkv_b': 8.0,
     'L0_ffn_wo_w': 3.69,
     'L0_ffn_wo_b': 3.443,
     'L1_attn_Wq': 8.0,
     'L1_attn_Wk': 8.0,
     'L1_ffn_gate_w': 5.804,
     'L1_ffn_w1': 8.0,
     'L1_ffn_w2': 8.0}
    for name, (base, spread) in spreads.items():
        noise = np.random.default_rng([zlib.crc32(name.encode()), seed]).standard_normal(out[name].shape)
        drawn = base * np.exp(spread * noise) if base else spread * noise
        out[name] = jnp.asarray(drawn.astype(out[name].dtype))
    for name, factor in factors.items():
        out[name] = (out[name] * factor).astype(out[name].dtype)
    return out
```

```python
from contextlib import ExitStack

import concourse.bass as bass
from concourse import mybir

F32 = mybir.dt.float32
BF16 = mybir.dt.bfloat16
I32 = mybir.dt.int32
U32 = mybir.dt.uint32
ALU = mybir.AluOpType
ACT = mybir.ActivationFunctionType
AX = mybir.AxisListType

P = 128
HP, PATCH = 4, 8
LN_SETS = "natural_log_exp_and_others"


class Round:

    def __init__(self, nc, tag, names, units, dma=()):
        self.nc, self.units = nc, units
        self.s = {n: nc.alloc_semaphore(name=f"{tag}_{n}") for n in (*names, *dma)}
        for n in names:
            nc.gpsimd.sem_inc(self.s[n], units)
        for n in dma:
            nc.gpsimd.sem_inc(self.s[n], 16)
        nc.all_engine_barrier()

    def __getitem__(self, name):
        return self.s[name]

    def now(self, i, u=0):
        return i * self.units + (u + 1)

    def before(self, i, u=0):
        return i * self.units + (u + 1 - self.units) if u + 1 != self.units else i * self.units

    def close(self):
        self.nc.all_engine_barrier()
        self.nc.clear_and_free_semaphores(list(self.s.values()))
        self.nc.all_engine_barrier()


def loaded(i):
    return i * 16 + 16


def weave(*engine_steps):
    waiting = [[at, n, g] for n, g in enumerate(engine_steps) for at in (next(g, None),) if at is not None]
    while waiting:
        first = min(waiting, key=lambda w: (w[0], w[1]))
        try:
            first[0] = next(first[2])
        except StopIteration:
            waiting.remove(first)


def sent(i):
    return i * 16


def across(ap, axis, count):
    shape = list(ap.shape)
    shape.insert(axis, count)
    return ap.unsqueeze(axis).to_broadcast(shape)


class Core:

    LOW = -44.0

    def __init__(self, nc, ctx, dram, images):
        self.nc, self.dram, self.N = nc, dram, images
        self.G = (104 // PATCH)
        self.NT = self.G * self.G
        self.T = images * self.NT
        self.H = ctx.enter_context(nc.sbuf_tensor("H", [P, self.T], F32))
        self.cols = ctx.enter_context(nc.sbuf_tensor("cols", [P, dram["cols"].shape[1]], F32))
        self.ident = ctx.enter_context(nc.sbuf_tensor("ident", [P, P], F32))
        self.avg = ctx.enter_context(nc.sbuf_tensor("avg", [P, P], F32))
        self.eps = ctx.enter_context(nc.sbuf_tensor("eps", [P, 4], F32))
        self.passed = nc.alloc_semaphore(name="passed")

    def col(self, name, k=0):
        c = COLS[name][0] + k
        return self.cols[:, c:c + 1]

    def image(self, i, u, units):
        return bass.ds(i * (units * self.NT) + (u - units) * self.NT, self.NT)


COLS = {}
_c = 0
for _name, _n in (("tok_b", 1), ("conv_b", 2), ("dt_b", 2), ("D", 2), ("n1g", 1), ("n1b", 1), ("n2g", 1), ("n2b", 1),
                  ("n3g", 1), ("n3b", 1), ("ang", 1), ("anb", 1), ("wq_b", 1), ("wk_b", 1), ("wv_b", 1), ("wo_b", 1),
                  ("gate_b", 1), ("f_b1", 4), ("f_b2", 1), ("pos_w", 3), ("pos_b", 1), ("q2_b", 1), ("k2_b", 1),
                  ("v2_b", 1), ("o2_b", 1), ("q3_b", 1), ("k3_b", 1), ("v3_b", 1), ("o3_b", 1), ("g3", 1), ("b3", 1),
                  ("sb1", 4), ("sb2", 1), ("eb1", 64), ("eb2", 16)):
    COLS[_name] = (_c, _n)
    _c += _n
COLS_WIDTH = _c


def constants(c):
    nc = c.nc
    r = Round(nc, "cst", ["made", "filled"], 1, dma=["cols"])
    with nc.Block() as block:
        @block.sync
        def _(sp):
            sp.dma_start(c.cols[:, :], c.dram["cols"]).then_inc(r["cols"], 16)
            sp.wait_ge(r["cols"], 32)

        @block.gpsimd
        def _(pool):
            nc.gpsimd.memset(c.avg[:, :], 1.0 / P)
            nc.gpsimd.memset(c.eps[:, 0:1], 1e-5)
            nc.gpsimd.memset(c.eps[:, 1:2], 1e-7)
            nc.gpsimd.memset(c.eps[:, 2:3], 1e-3)
            nc.gpsimd.memset(c.eps[:, 3:4], 1.0)
            nc.gpsimd.memset(c.ident[:, :], 0.0).then_inc(r["made"], 1)
            pool.wait_ge(r["made"], 2)
            nc.gpsimd.affine_select(out=c.ident[:, :], in_=c.ident[:, :], compare_op=ALU.not_equal, fill=1.0, base=0,
                                    pattern=[[-1, P]], channel_multiplier=1).then_inc(r["filled"], 1)
    r.close()


def tokens_stage(c):
    nc, NT, G, N, T = c.nc, c.NT, c.G, c.N, c.T
    V, PAIR, SLOTS = 5, 2, 2
    O = G + 1
    COUNT = float(V * 2 * (G * PATCH) ** 2)
    rounds = N // (PAIR * SLOTS)
    names = ["stats", "xg_v", "xg_p", "mm", "kept", "gwb", "fin", "fin_mm", "fin_a"]
    r = Round(nc, "tok", names, SLOTS, dma=["w", "gam", "bet", "xb0", "xb1", "xo0", "xo1"])
    ctx = ExitStack()
    with ctx:
        sb = lambda n, s, d=F32: ctx.enter_context(nc.sbuf_tensor("tok_" + n, s, d))
        W = sb("tokW", [P, V, P])
        gam = sb("gam", [P, V, NT])
        bet = sb("bet", [P, V, NT])
        xb = sb("xb", [P, SLOTS, PAIR, NT])
        xo = sb("xo", [P, SLOTS, PAIR, O * O])
        xg = sb("xg", [P, SLOTS, V, PAIR, NT])
        st = sb("st", [P, N, V * 6])
        sm = sb("sm", [P, N, V * 2])
        s1 = sb("s1", [P, 2, N])
        pm = [ctx.enter_context(nc.psum_tensor(f"pm{k}", [P, 512], F32)) for k in range(SLOTS)]
        pw = ctx.enter_context(nc.psum_tensor("pw", [P, 2, 256], F32))
        pf = ctx.enter_context(nc.psum_tensor("pf", [P, 2, 256], F32))

        def view(s, v, b=None):
            lo = lambda z: slice(z, z + G)
            if v == 0:
                x = xb[:, s, :, :].rearrange("p b (h w) -> p b h w", h=G)
                return x if b is None else x[:, b]
            h, w = ((1, 0), (1, 1), (0, 0), (0, 1))[v - 1]
            x = xo[:, s, :, :].rearrange("p b (h w) -> p b h w", h=O)[:, :, lo(h), lo(w)]
            return x if b is None else x[:, b]

        with nc.Block() as block:
            @block.sync
            def _(sp):
                sp.dma_start(W[:, :, :], c.dram["tokW"]).then_inc(r["w"], 16)
                sp.dma_start(gam[:, :, :], c.dram["gamma"]).then_inc(r["gam"], 16)
                sp.dma_start(bet[:, :, :], c.dram["beta"]).then_inc(r["bet"], 16)
                with sp.Fori(1, rounds + 1) as i:
                    for s in range(SLOTS):
                        at = bass.ds(sp.snap(i * (PAIR * SLOTS) + (s - SLOTS) * PAIR), PAIR)
                        read = sp.snap(r.before(i, s))
                        sp.wait_ge(r["stats"], read)
                        sp.wait_ge(r["xg_p"], read)
                        sp.wait_ge(r["xg_v"], read)
                        sp.dma_start(xb[:, s], c.dram["xbase"][:, at, :]).then_inc(r[f"xb{s}"], 16)
                        sp.dma_start(xo[:, s], c.dram["xoff"][:, at, :]).then_inc(r[f"xo{s}"], 16)

            def weigh(eng, i, s, v):
                g = across(gam[:, v, :].rearrange("p (h w) -> p h w", h=G), 1, PAIR)
                o = xg[:, s, v].rearrange("p b (h w) -> p b h w", h=G)
                return eng.tensor_tensor(o, view(s, v), g, ALU.mult)

            @block.gpsimd
            def _(pool):
                pool.wait_ge(r["gam"], 32)
                with pool.Fori(1, rounds + 1) as i:
                    for s in range(SLOTS):
                        pool.wait_ge(r[f"xb{s}"], loaded(i))
                        pool.wait_ge(r[f"xo{s}"], loaded(i))
                        pool.wait_ge(r["mm"], r.before(i, s))
                        weigh(nc.gpsimd, i, s, 3)
                        weigh(nc.gpsimd, i, s, 4).then_inc(r["xg_p"], 1)

            @block.vector
            def _(dve):
                dve.wait_ge(r["gam"], 32)
                with dve.Fori(1, rounds + 1) as i:
                    for s in range(SLOTS):
                        dve.wait_ge(r[f"xb{s}"], loaded(i))
                        dve.wait_ge(r[f"xo{s}"], loaded(i))
                        dve.wait_ge(r["mm"], r.before(i, s))
                        for v in range(3):
                            last = weigh(nc.vector, i, s, v)
                        last.then_inc(r["xg_v"], 1)
                        for b in range(PAIR):
                            at = bass.ds(i * (PAIR * SLOTS) + (s - SLOTS) * PAIR + b, 1)
                            for v in range(V):
                                last = nc.vector.bn_stats(st[:, at, v * 6:v * 6 + 6], view(s, v, b))
                        last.then_inc(r["stats"], 1)
                k = [r.units]

                def step(ins):
                    k[0] += 1
                    ins.then_inc(r["fin"], 1)
                    dve.wait_ge(r["fin"], k[0])
                cell = st[:, :, :].rearrange("p n (v m) -> p n v m", m=3)
                cnt, mean, m2 = cell[:, :, :, 0], cell[:, :, :, 1], cell[:, :, :, 2]
                dve.wait_ge(r["stats"], r.now(rounds, SLOTS - 1))
                step(nc.vector.tensor_tensor(sm[:, :, :], cnt, mean, ALU.mult))
                step(nc.vector.tensor_reduce(s1[:, 0, :], sm[:, :, :], AX.X, ALU.add))
                dve.wait_ge(r["fin_mm"], SLOTS + 1)
                step(nc.vector.tensor_scalar(s1[:, 0, :], pf[:, 0, 0:N], float(P) / COUNT, None, ALU.mult))
                step(nc.vector.tensor_tensor(mean, mean, across(s1[:, 0, :], 2, V * 2), ALU.subtract))
                step(nc.vector.tensor_tensor(sm[:, :, :], cnt, mean, ALU.mult))
                step(nc.vector.tensor_tensor(sm[:, :, :], sm[:, :, :], mean, ALU.mult))
                step(nc.vector.tensor_tensor(sm[:, :, :], sm[:, :, :], m2, ALU.add))
                step(nc.vector.tensor_reduce(s1[:, 1, :], sm[:, :, :], AX.X, ALU.add))
                dve.wait_ge(r["fin_a"], SLOTS + 2)
                step(nc.vector.scalar_tensor_tensor(c.nmr[:, :], s1[:, 0, :], -1.0, c.rstd[:, :], ALU.mult, ALU.mult))

            @block.tensor
            def _(pe):
                pe.wait_ge(r["w"], 32)
                pe.wait_ge(r["gam"], 32)
                pe.wait_ge(r["bet"], 32)
                for a, t in enumerate((gam, bet)):
                    for v in range(V):
                        last = nc.tensor.matmul(pw[:, a, 0:NT], W[:, v, :], t[:, v, :], start=(v == 0), stop=(v == V - 1))
                last.then_inc(r["gwb"], 1)
                with pe.Fori(1, rounds + 1) as i:
                    for s in range(SLOTS):
                        pe.wait_ge(r["xg_v"], r.now(i, s))
                        pe.wait_ge(r["xg_p"], r.now(i, s))
                        pe.wait_ge(r["kept"], r.before(i, s))
                        for v in range(V):
                            last = nc.tensor.matmul(pm[s][:, 0:PAIR * NT], W[:, v, :],
                                                    xg[:, s, v].rearrange("p b t -> p (b t)"),
                                                    start=(v == 0), stop=(v == V - 1))
                        last.then_inc(r["mm"], 1)
                pe.wait_ge(r["fin"], SLOTS + 2)
                nc.tensor.matmul(pf[:, 0, 0:N], c.avg[:, :], s1[:, 0, :], start=True, stop=True).then_inc(r["fin_mm"], 1)
                pe.wait_ge(r["fin"], SLOTS + 8)
                nc.tensor.matmul(pf[:, 1, 0:N], c.avg[:, :], s1[:, 1, :], start=True, stop=True).then_inc(r["fin_mm"], 1)

            @block.scalar
            def _(act):
                act.wait_ge(r["gwb"], SLOTS + 1)
                nc.scalar.activation(c.gw[:, :], pw[:, 0, 0:NT], ACT.Copy)
                nc.scalar.activation(c.bw[:, :], pw[:, 1, 0:NT], ACT.Identity, bias=c.col("tok_b"))
                with act.Fori(1, rounds + 1) as i:
                    for s in range(SLOTS):
                        act.wait_ge(r["mm"], r.now(i, s))
                        at = bass.ds(i * (PAIR * SLOTS * NT) + (s - SLOTS) * PAIR * NT, PAIR * NT)
                        nc.scalar.activation(c.H[:, at], pm[s][:, 0:PAIR * NT], ACT.Copy).then_inc(r["kept"], 1)
                nc.scalar.preload_act_table_set(LN_SETS)
                act.wait_ge(r["fin_mm"], SLOTS + 2)
                nc.scalar.activation(c.rstd[:, :], pf[:, 1, 0:N], ACT.Ln, bias=c.eps[:, 1:2], scale=float(P) / COUNT).then_inc(r["fin_a"], 1)
                act.wait_ge(r["fin_a"], SLOTS + 1)
                nc.scalar.activation(c.rstd[:, :], c.rstd[:, :], ACT.Exp, scale=-0.5).then_inc(r["fin_a"], 1)
        r.close()


def mamba_stage(c):
    nc, NT, N = c.nc, c.NT, c.N
    S, HALF, TAPS, PARTS, SLOTS = 16, 2, 4, 3, 2
    GN = 3
    groups = [(n, min(GN, S - n)) for n in range(0, S, GN)]
    NG, BANKS, SC = len(groups), 4, 8
    LT = NT + 1
    names = ["h_shift", "h", "mean", "xc", "sq", "var", "lnv", "rstd", "xn", "xnp", "proj", "res", "e", "e1", "lne", "rec",
             "u", "sres", "dt", "bc", "absz", "expz", "softp", "relu_z", "delta", "du", "hi", "rest", "mid",
             "parts", "out", "mo", "yd", "yg", "ysum_most", "ysum", "chdone"]
    LATE = 4
    r = Round(nc, "mam", names, 1, dma=["mo_out"])
    pbs = Round(nc, "mamg", ["rows", "read", "da"], 2 * NG)
    scn = Round(nc, "mams", ["dbu", "scan", "ch"], NG)
    das = Round(nc, "mamd", ["da"], S)
    AIDED = (3, 4)
    NA = len(AIDED)
    aid = Round(nc, "mama", ["copied", "multiplied"], 2 * NA)
    pre = Round(nc, "mamp", ["clear", "cst", "sel"], 1, dma=["w"])
    ctx = ExitStack()
    with ctx:
        sb = lambda n, s, d=F32: ctx.enter_context(nc.sbuf_tensor("mam_" + n, s, d))
        ps = lambda n, s, d=F32: ctx.enter_context(nc.psum_tensor("mam_" + n, s, d))
        wm = sb("wm", [P, HALF * P])
        wk = sb("wk", [P, TAPS, HALF * P])
        wr = sb("wr", [P, HALF * P])
        wx = sb("wx", [P, HALF, PARTS * 2 * S])
        wdt = sb("wdt", [P, HALF, HALF * P])
        wout = sb("wout", [P, HALF, P])
        A = sb("A", [P, S])
        pick = sb("pick", [PARTS * 2 * S, 2 * S, P], BF16)
        dA = sb("dA", [P, HALF, S, LT])
        dB = sb("dB", [P, HALF, S, LT])
        xc, sq, rs = sb("xc", [P, NT]), sb("sq", [P, NT]), sb("rs", [P, NT])
        xnp = sb("xnp", [P, TAPS - 1 + NT])
        eu = sb("eu", [P, 2, HALF, NT])
        u_ = sb("u_", [P, SLOTS, HALF, NT])
        sres = sb("sres", [P, SLOTS, HALF, NT])
        az, mz = sb("az", [P, HALF, NT]), sb("mz", [P, HALF, NT])
        delta, du = sb("delta", [P, SLOTS, HALF, NT]), sb("du", [P, SLOTS, HALF, NT])
        bc3 = sb("bc3", [PARTS * 2 * S, SLOTS, NT], BF16)
        r1 = sb("r1", [PARTS * 2 * S, NT])
        r2 = sb("r2", [PARTS * 2 * S, NT], BF16)
        yd = sb("yd", [P, HALF, NT])
        yg = sb("yg", [P, HALF, NT])
        mo = sb("mo", [P, NT])
        brow = sb("brow", [P, NA, GN, NT])
        pl = ps("pl", [P, 2, 256])
        pa = ps("pa", [P, HALF, 256])
        pr = ps("pr", [P, HALF, 256])
        pb = [ps(f"pb{k}", [P, GN, NT]) for k in range(BANKS)]
        py = ps("py", [P, GN, NT])
        img = lambda m: bass.ds(m * NT - NT, NT)

        with nc.Block() as block:
            @block.sync
            def _(sp):
                loads = ((wm[:, :], c.dram["w_in"][:, 0:HALF * P]), (wr[:, :], c.dram["w_in"][:, HALF * P:]),
                         (wk[:, :, :], c.dram["taps"]), (wdt[:, :, :], c.dram["w_dt"]), (wout[:, :, :], c.dram["w_out"]),
                         (A[:, :], c.dram["A_log"]),
                         *((wx[:, :, k * 2 * S:(k + 1) * 2 * S], c.dram["w_x"]) for k in range(PARTS)))
                for k, (t, s) in enumerate(loads):
                    sp.dma_start(t, s).then_inc(pre["w"], 16)
                    sp.wait_ge(pre["w"], 32 + 16 * k)

        with nc.Block() as block:
            @block.gpsimd
            def _(pool):
                nc.gpsimd.memset(pick[:, :, :], 0.0).then_inc(pre["clear"], 1)
                for k in range(PARTS):
                    pool.wait_ge(pre["clear"], 2 + k)
                    nc.gpsimd.affine_select(out=pick[:, :, :], in_=pick[:, :, :], compare_op=ALU.not_equal, fill=1.0,
                                            base=-2 * S * k, pattern=[[-1, 2 * S], [0, P]],
                                            channel_multiplier=1).then_inc(pre["clear"], 1)
                nc.gpsimd.memset(xnp[:, 0:TAPS - 1], 0.0)
                for t in (dA, dB):
                    nc.gpsimd.memset(t[:, :, :, 0:1], 0.0)

            @block.vector
            def _(dve):
                nc.vector.tensor_tensor(wk[:, :, :], wk[:, :, :], across(wm[:, :], 1, TAPS), ALU.mult)
                dve.wait_ge(pre["sel"], 2)
                nc.vector.tensor_scalar(A[:, :], A[:, :], -1.0, None, ALU.mult)

            @block.scalar
            def _(act):
                nc.scalar.preload_act_table_set(LN_SETS)
                nc.scalar.activation(A[:, :], A[:, :], ACT.Exp).then_inc(pre["sel"], 1)

        with nc.Block() as block:
            @block.sync
            def _(sp):
                with sp.Fori(1, N + 1) as m:
                    at = sp.snap(m * NT - NT)
                    sp.wait_ge(r["mo"], m + 1)
                    sp.dma_start(c.mo_dram[:, bass.ds(at, NT)], mo[:, :]).then_inc(r["mo_out"], 16)
                sp.wait_ge(r["mo_out"], loaded(N))

            @block.gpsimd
            def _(pool):
                def prepare(m, s):
                    yield 1
                    pool.wait_ge(r["xc"], m + 1)
                    pool.wait_ge(r["var"], m)
                    nc.gpsimd.tensor_tensor(sq[:, :], xc[:, :], xc[:, :], ALU.mult).then_inc(r["sq"], 1)
                    yield 1.93
                    pool.wait_ge(r["rstd"], m + 1)
                    pool.wait_ge(r["sq"], m + 1)
                    nc.gpsimd.tensor_tensor(xc[:, :], xc[:, :], rs[:, :], ALU.mult).then_inc(r["xn"], 1)
                    yield 25
                    pool.wait_ge(r["relu_z"], m + 1)
                    pool.wait_ge(r["softp"], m + 1)
                    nc.gpsimd.tensor_tensor(delta[:, s], mz[:, :, :], az[:, :, :], ALU.add).then_inc(r["delta"], 1)
                    yield 25.6
                    pool.wait_ge(r["delta"], m + 1)
                    pool.wait_ge(r["u"], m + 1)
                    nc.gpsimd.tensor_tensor(du[:, s], delta[:, s], u_[:, s], ALU.mult).then_inc(r["du"], 1)

                def scan(m, s):
                    for u, k in enumerate(AIDED):
                        n0, n = groups[k]
                        yield 3.2 + 1.5 * u
                        pool.wait_ge(aid["copied"], aid.now(m, u))
                        pool.wait_ge(aid["multiplied"], aid.now(m, u) - NA)
                        pool.wait_ge(r["du"], m + 1)
                        nc.gpsimd.tensor_tensor(dB[:, :, n0:n0 + n, 1:LT], across(du[:, s], 2, n),
                                                across(brow[:, u, 0:n, :], 1, HALF), ALU.mult).then_inc(aid["multiplied"], 1)
                    for u, k in enumerate(AIDED):
                        n0, n = groups[k]
                        yield 19.2 + 1.5 * u
                        pool.wait_ge(aid["copied"], aid.now(m, NA + u))
                        pool.wait_ge(r["chdone"], m + 1)
                        nc.gpsimd.tensor_tensor(dA[:, :, n0:n0 + n, 1:LT], dB[:, :, n0:n0 + n, 1:LT],
                                                across(brow[:, u, 0:n, :], 1, HALF), ALU.mult).then_inc(aid["multiplied"], 1)

                def finish(m, s):
                    yield 10
                    pool.wait_ge(r["yd"], m + 1)
                    pool.wait_ge(r["out"], m)
                    nc.gpsimd.tensor_tensor(yg[:, :, :], yd[:, :, :], sres[:, s], ALU.mult).then_inc(r["yg"], 1)
                drive(c, pool, prepare, scan, finish)

            @block.tensor
            def _(pe):
                def prepare(m, s):
                    yield 1
                    pe.wait_ge(r["h"], m + 1)
                    pe.wait_ge(r["xc"], m)
                    nc.tensor.matmul(pl[:, 0, 0:NT], c.avg[:, :], c.H[:, img(m)], start=True, stop=True).then_inc(r["mean"], 1)
                    yield 2
                    pe.wait_ge(r["sq"], m + 1)
                    pe.wait_ge(r["lnv"], m)
                    nc.tensor.matmul(pl[:, 1, 0:NT], c.avg[:, :], sq[:, :], start=True, stop=True).then_inc(r["var"], 1)
                    yield 7.5
                    pe.wait_ge(r["xnp"], m + 1)
                    pe.wait_ge(r["relu_z"], m)
                    pe.wait_ge(r["absz"], m)
                    for h in range(HALF):
                        for k in range(TAPS):
                            last = nc.tensor.matmul(pa[:, h, 0:NT], wk[:, k, h * P:(h + 1) * P], xnp[:, k:k + NT],
                                                    start=(k == 0), stop=(k == TAPS - 1))
                    last.then_inc(r["proj"], 1)
                    pe.wait_ge(r["hi"], m)
                    pe.wait_ge(r["rest"], m)
                    for h in range(HALF):
                        last = nc.tensor.matmul(pr[:, h, 0:NT], wr[:, h * P:(h + 1) * P], xnp[:, TAPS - 1:], start=True, stop=True)
                    last.then_inc(r["res"], 1)
                    yield 17.55
                    pe.wait_ge(r["u"], m + 1)
                    for h in range(HALF):
                        for k in range(HALF):
                            last = nc.tensor.matmul(pa[:, h, 0:NT], wdt[:, k, h * P:(h + 1) * P], u_[:, s, k, :],
                                                    start=(k == 0), stop=(k == HALF - 1))
                    last.then_inc(r["dt"], 1)
                    pe.wait_ge(r["sres"], m + 1)
                    for k in range(HALF):
                        last = nc.tensor.matmul(pr[0:PARTS * 2 * S, 0, 0:NT], wx[:, k, :], u_[:, s, k, :],
                                                start=(k == 0), stop=(k == HALF - 1))
                    last.then_inc(r["bc"], 1)

                def scan(m, s):
                    def rows(k, first):
                        n0, n = groups[k]
                        q = k + (NG if first else 0)
                        pe.wait_ge(pbs["read"], m * (2 * NG) + (q + 1 - BANKS))
                        for a in range(n):
                            last = nc.tensor.matmul(pb[q % BANKS][:, a, :], pick[:, first + n0 + a, :], bc3[:, s, :],
                                                    start=True, stop=True)
                        last.then_inc(pbs["rows"], 1)
                    yield 0
                    pe.wait_ge(r["parts"], m + 1)
                    for k in range(NG):
                        yield 0.1 + k
                        rows(k, 0)
                    for k in range(BANKS):
                        yield 9 + k
                        rows(k, S)
                    for k in range(LATE):
                        yield 19.5 + k
                        if k + BANKS < NG:
                            rows(k + BANKS, S)
                        total(m, k)
                    yield 28

                def total(m, k):
                    n0, n = groups[k]
                    if k in AIDED:
                        pe.wait_ge(aid["multiplied"], aid.now(m, NA + AIDED.index(k)))
                    else:
                        pe.wait_ge(scn["ch"], scn.now(m, k))
                    if k == 0:
                        pe.wait_ge(r["yd"], m)
                        pe.wait_ge(r["mo"], m)
                    for n_ in range(n0, n0 + n):
                        last = nc.tensor.matmul(py[:, 0:HALF, :], c.ident[:, :], dA[:, :, n_, 1:LT],
                                                start=(n_ == 0), stop=(n_ == S - 1))
                    if k in (LATE - 1, NG - 1):
                        last.then_inc(r["ysum_most" if k < LATE else "ysum"], 1)

                def finish(m, s):
                    for k in range(LATE, NG):
                        yield 4.05 + (k - LATE)
                        total(m, k)
                    yield 12.5
                    pe.wait_ge(r["yg"], m + 1)
                    for k in range(HALF):
                        last = nc.tensor.matmul(py[:, HALF, :], wout[:, k, :], yg[:, k, :], start=(k == 0), stop=(k == HALF - 1))
                    last.then_inc(r["out"], 1)
                drive(c, pe, prepare, scan, finish)

            @block.scalar
            def _(act):
                def prepare(m, s):
                    yield 2
                    act.wait_ge(r["var"], m + 1)
                    act.wait_ge(r["xn"], m)
                    nc.scalar.activation(rs[:, :], pl[:, 1, 0:NT], ACT.Ln, bias=c.eps[:, 0:1]).then_inc(r["lnv"], 1)
                    yield 2.5
                    act.wait_ge(r["lnv"], m + 1)
                    nc.scalar.activation(rs[:, :], rs[:, :], ACT.Exp, scale=-0.5).then_inc(r["rstd"], 1)
                    yield 3.52
                    act.wait_ge(r["xn"], m + 1)
                    act.wait_ge(r["res"], m)
                    nc.scalar.activation(xnp[:, TAPS - 1:], xc[:, :], ACT.Identity, scale=c.col("n1g"), bias=c.col("n1b")).then_inc(r["xnp"], 1)
                    yield 10.2
                    act.wait_ge(r["e1"], m + 1)
                    nc.scalar.activation(eu[:, :, :, :], eu[:, :, :, :], ACT.Exp, scale=-1.0).then_inc(r["e"], 1)
                    yield 10.3
                    act.wait_ge(r["e"], m + 1)
                    nc.scalar.activation(eu[:, :, :, :], eu[:, :, :, :], ACT.Ln, bias=c.eps[:, 3:4]).then_inc(r["lne"], 1)
                    yield 10.4
                    act.wait_ge(r["lne"], m + 1)
                    nc.scalar.activation(eu[:, :, :, :], eu[:, :, :, :], ACT.Exp, scale=-1.0).then_inc(r["rec"], 1)
                    yield 24.1
                    act.wait_ge(r["dt"], m + 1)
                    act.wait_ge(r["delta"], m)
                    for h in range(HALF):
                        last = nc.scalar.activation(az[:, h, :], pa[:, h, 0:NT], ACT.Abs, bias=c.col("dt_b", h))
                    last.then_inc(r["absz"], 1)
                    for h in range(HALF):
                        last = nc.scalar.activation(mz[:, h, :], pa[:, h, 0:NT], ACT.Relu, bias=c.col("dt_b", h))
                    last.then_inc(r["relu_z"], 1)
                    yield 24.3
                    act.wait_ge(r["absz"], m + 1)
                    nc.scalar.activation(az[:, :, :], az[:, :, :], ACT.Exp, scale=-1.0).then_inc(r["expz"], 1)
                    yield 24.4
                    act.wait_ge(r["expz"], m + 1)
                    nc.scalar.activation(az[:, :, :], az[:, :, :], ACT.Ln, bias=c.eps[:, 3:4]).then_inc(r["softp"], 1)

                def scan(m, s):
                    yield 0
                    act.wait_ge(r["delta"], m + 1)
                    act.wait_ge(r["ysum_most"], m)
                    def copy(u, q):
                        n = groups[AIDED[u % NA]][1]
                        act.wait_ge(pbs["rows"], m * (2 * NG) + q + 1)
                        act.wait_ge(aid["multiplied"], aid.now(m, u) - NA)
                        nc.scalar.activation(brow[:, u % NA, 0:n, :], pb[q % BANKS][:, 0:n, :], ACT.Copy).then_inc(aid["copied"], 1)
                    for n in range(S):
                        yield 0.1 + 0.5 * n
                        if n in (5, 7):
                            copy((n - 5) // 2, AIDED[(n - 5) // 2])
                        if n == groups[LATE][0]:
                            act.wait_ge(r["ysum"], m)
                        nc.scalar.activation(dA[:, :, n, 1:LT], delta[:, s], ACT.Exp, scale=A[:, n:n + 1]).then_inc(das["da"], 1)
                    for u, k in enumerate(AIDED):
                        yield 18 + 2.2 * u
                        copy(NA + u, NG + k)

                def finish(m, s):
                    yield 13.3
                    act.wait_ge(r["out"], m + 1)
                    act.wait_ge(r["mo_out"], sent(m))
                    nc.scalar.activation(mo[:, :], py[:, HALF, :], ACT.Copy).then_inc(r["mo"], 1)
                nc.scalar.preload_act_table_set(LN_SETS)
                drive(c, act, prepare, scan, finish)

            @block.vector
            def _(dve):
                def prepare(m, s):
                    yield 0
                    dve.wait_ge(r["xnp"], m)
                    one = bass.ds(m - 1, 1)
                    nc.vector.scalar_tensor_tensor(xc[:, :], c.gw[:, :], c.nmr[:, one], c.bw[:, :], ALU.mult, ALU.add).then_inc(r["h_shift"], 1)
                    yield 0
                    dve.wait_ge(r["h_shift"], m + 1)
                    nc.vector.scalar_tensor_tensor(c.H[:, img(m)], c.H[:, img(m)], c.rstd[:, one], xc[:, :], ALU.mult, ALU.add).then_inc(r["h"], 1)
                    yield 2
                    dve.wait_ge(r["mean"], m + 1)
                    dve.wait_ge(r["h"], m + 1)
                    nc.vector.tensor_tensor(xc[:, :], c.H[:, img(m)], pl[:, 0, 0:NT], ALU.subtract).then_inc(r["xc"], 1)
                    yield 10.1
                    dve.wait_ge(r["proj"], m + 1)
                    for h in range(HALF):
                        nc.vector.tensor_scalar(eu[:, 0, h, :], pa[:, h, 0:NT], c.col("conv_b", h), c.LOW, ALU.add, ALU.max)
                    dve.wait_ge(r["res"], m + 1)
                    nc.vector.tensor_scalar(eu[:, 1, :, :], pr[:, :, 0:NT], c.LOW, None, ALU.max).then_inc(r["e1"], 1)
                    yield 17.5
                    dve.wait_ge(r["rec"], m + 1)
                    old(dve, r["yd"], m - 1)
                    old(dve, r["yg"], m - 1)
                    for h in range(HALF):
                        last = nc.vector.scalar_tensor_tensor(u_[:, s, h, :], pa[:, h, 0:NT], c.col("conv_b", h), eu[:, 0, h, :], ALU.add, ALU.mult)
                    last.then_inc(r["u"], 1)
                    yield 17.6
                    nc.vector.tensor_tensor(sres[:, s], pr[:, :, 0:NT], eu[:, 1], ALU.mult).then_inc(r["sres"], 1)
                    yield 24.3
                    dve.wait_ge(r["bc"], m + 1)
                    q = 2 * S
                    nc.vector.tensor_copy(bc3[:, s, :], pr[0:PARTS * q, 0, 0:NT]).then_inc(r["hi"], 1)
                    yield 26.4
                    dve.wait_ge(r["hi"], m + 1)
                    nc.vector.tensor_tensor(r1[:, :], pr[0:PARTS * q, 0, 0:NT], bc3[:, s, :], ALU.subtract).then_inc(r["rest"], 1)
                    yield 25.84
                    dve.wait_ge(r["rest"], m + 1)
                    nc.vector.tensor_copy(r2[:, :], r1[:, :]).then_inc(r["mid"], 1)
                    yield 24.6
                    dve.wait_ge(r["mid"], m + 1)
                    nc.vector.tensor_copy(bc3[q:2 * q, s, :], r2[q:2 * q, :])
                    nc.vector.tensor_tensor(bc3[2 * q:, s, :], r1[2 * q:, :], r2[2 * q:, :], ALU.subtract).then_inc(r["parts"], 1)

                def scan(m, s):
                    yield 0
                    dve.wait_ge(r["du"], m + 1)
                    dve.wait_ge(scn["ch"], scn.now(m, NG - 1) - NG)
                    for k, (n0, n) in enumerate(groups):
                        yield 2.1 + k
                        if k in AIDED:
                            dve.wait_ge(aid["copied"], aid.now(m, AIDED.index(k)))
                            dve.sem_inc(scn["dbu"], 1)
                            dve.sem_inc(pbs["read"], 1)
                            continue
                        dve.wait_ge(pbs["rows"], m * (2 * NG) + k + 1)
                        nc.vector.tensor_tensor(dB[:, :, n0:n0 + n, 1:LT], across(du[:, s], 2, n),
                                                across(pb[k % BANKS][:, 0:n, :], 1, HALF), ALU.mult).then_inc(scn["dbu"], 1)
                        dve.wait_ge(scn["dbu"], scn.now(m, k))
                        dve.sem_inc(pbs["read"], 1)
                    for q in range(S // SC):
                        for h in range(HALF):
                            yield 9 + 3 * (q * HALF + h)
                            dve.wait_ge(das["da"], das.now(m, (q + 1) * SC - 1))
                            if q:
                                dve.wait_ge(aid["multiplied"], aid.now(m, NA - 1))
                            flat = lambda t: t[:, h, q * SC:(q + 1) * SC, :].rearrange("p n t -> p (n t)")
                            last = nc.vector.tensor_tensor_scan(flat(dB), flat(dA), flat(dB), 0.0, ALU.mult, ALU.add)
                    last.then_inc(r["chdone"], 1)
                    dve.wait_ge(r["chdone"], m + 1)
                    for k, (n0, n) in enumerate(groups):
                        yield 19 + k
                        if k in AIDED:
                            dve.wait_ge(aid["copied"], aid.now(m, NA + AIDED.index(k)))
                            dve.sem_inc(scn["ch"], 1)
                            dve.sem_inc(pbs["read"], 1)
                            continue
                        dve.wait_ge(pbs["rows"], m * (2 * NG) + NG + k + 1)
                        nc.vector.tensor_tensor(dA[:, :, n0:n0 + n, 1:LT], dB[:, :, n0:n0 + n, 1:LT],
                                                across(pb[(NG + k) % BANKS][:, 0:n, :], 1, HALF), ALU.mult).then_inc(scn["ch"], 1)
                        dve.wait_ge(scn["ch"], scn.now(m, k))
                        dve.sem_inc(pbs["read"], 1)

                def finish(m, s):
                    yield 6.33
                    dve.wait_ge(r["ysum"], m + 1)
                    dve.wait_ge(r["yg"], m)
                    for h in range(HALF):
                        last = nc.vector.scalar_tensor_tensor(yd[:, h, :], u_[:, s, h, :], c.col("D", h), py[:, h, :], ALU.mult, ALU.add)
                    last.then_inc(r["yd"], 1)
                drive(c, dve, prepare, scan, finish)
        for x in (r, pbs, scn, das, aid, pre):
            x.close()


class Norm:

    NAMES = ("mean", "xc", "sq", "var", "lnv", "rstd", "xn", "out")

    def __init__(self, c, r, ctx, tag, bank, eps, gain=None, offset=None):
        self.c, self.r, self.tag, self.bank, self.eps, self.gain, self.offset = c, r, tag, bank, eps, gain, offset
        self.xc, self.sq, self.rs = (ctx.enter_context(c.nc.sbuf_tensor(f"{tag}_{n}", [P, c.NT], F32)) for n in ("x", "s", "r"))

    @classmethod
    def names(cls, *tags):
        return [f"{t}_{n}" for t in tags for n in cls.NAMES]

    def at(self, name):
        return self.r[f"{self.tag}_{name}"]

    def pe(self, m, t, x, waits):
        c, NT = self.c, self.c.NT
        yield t
        for sem, value in waits:
            c.nc.tensor.wait_ge(sem, value)
        c.nc.tensor.matmul(self.bank[:, 0:NT], c.avg[:, :], x, start=True, stop=True).then_inc(self.at("mean"), 1)
        yield t + 3
        c.nc.tensor.wait_ge(self.at("sq"), m + 1)
        c.nc.tensor.matmul(self.bank[:, 256:256 + NT], c.avg[:, :], self.sq[:, :], start=True, stop=True).then_inc(self.at("var"), 1)

    def pool(self, m, t):
        yield t + 2
        self.c.nc.gpsimd.wait_ge(self.at("xc"), m + 1)
        self.c.nc.gpsimd.wait_ge(self.at("var"), m)
        self.c.nc.gpsimd.tensor_tensor(self.sq[:, :], self.xc[:, :], self.xc[:, :], ALU.mult).then_inc(self.at("sq"), 1)

    def act(self, m, t, out=None, waits=()):
        act, c = self.c.nc.scalar, self.c
        yield t + 4
        act.wait_ge(self.at("var"), m + 1)
        act.wait_ge(self.at("xn"), m)
        act.activation(self.rs[:, :], self.bank[:, 256:256 + c.NT], ACT.Ln, bias=self.eps).then_inc(self.at("lnv"), 1)
        act.wait_ge(self.at("lnv"), m + 1)
        act.activation(self.rs[:, :], self.rs[:, :], ACT.Exp, scale=-0.5).then_inc(self.at("rstd"), 1)
        if self.gain is not None:
            yield t + 6
            act.wait_ge(self.at("xn"), m + 1)
            for sem, value in waits:
                act.wait_ge(sem, value)
            act.activation(out, self.xc[:, :], ACT.Identity, scale=self.gain, bias=self.offset).then_inc(self.at("out"), 1)

    def dve(self, m, t, x, out=None, waits=()):
        dve, c = self.c.nc.vector, self.c
        yield t + 1
        dve.wait_ge(self.at("mean"), m + 1)
        if self.gain is not None:
            dve.wait_ge(self.at("out"), m)
        dve.tensor_tensor(self.xc[:, :], x, self.bank[:, 0:c.NT], ALU.subtract).then_inc(self.at("xc"), 1)
        yield t + 5
        dve.wait_ge(self.at("rstd"), m + 1)
        dve.wait_ge(self.at("sq"), m + 1)
        for sem, value in waits:
            dve.wait_ge(sem, value)
        dve.tensor_tensor(self.xc[:, :] if out is None else out, self.xc[:, :], self.rs[:, :], ALU.mult).then_inc(self.at("xn"), 1)


def drive(c, eng, prepare, heads, finish):
    N = c.N
    weave(prepare(1, 1))
    weave(prepare(2, 0), heads(1, 1))
    with eng.Fori(3, N, 2) as m:
        weave(prepare(m, 1), heads(m - 1, 0), finish(m - 2, 1))
        weave(prepare(m + 1, 0), heads(m, 1), finish(m - 1, 0))
    weave(heads(N, 0), finish(N - 1, 1))
    weave(finish(N, 0))


def drive_four(c, eng, prepare, heads, finish, mlp):
    N = c.N
    weave(prepare(1, 1))
    weave(prepare(2, 0), heads(1, 1))
    weave(prepare(3, 1), heads(2, 0), finish(1, 1))
    with eng.Fori(4, N - 1, 2) as m:
        weave(prepare(m, 0), heads(m - 1, 1), finish(m - 2, 0), mlp(m - 3, 1))
        weave(prepare(m + 1, 1), heads(m, 0), finish(m - 1, 1), mlp(m - 2, 0))
    weave(prepare(N, 0), heads(N - 1, 1), finish(N - 2, 0), mlp(N - 3, 1))
    weave(heads(N, 0), finish(N - 1, 1), mlp(N - 2, 0))
    weave(finish(N, 0), mlp(N - 1, 1))
    weave(mlp(N, 0))


class Heads:
    LO = 105
    NAMES = ("score", "mx", "exp", "z", "rz", "norm", "turned", "kept")
    BIG = -3.0e38

    def __init__(self, c, ctx, tag, many, top):
        self.c, self.many, self.top = c, many, top
        NT, LO = c.NT, self.LO
        self.KLO, self.KHI = P, NT - P
        sb = lambda n, s, d=F32: ctx.enter_context(c.nc.sbuf_tensor(f"{tag}_{n}", s, d))
        ps = lambda n, s: ctx.enter_context(c.nc.psum_tensor(f"{tag}_{n}", s, F32))
        if many:
            self.NH = 8
            lo = [(LO, [[(h, 0, LO, 0)] for h in (2 * g, 2 * g + 1)]) for g in range(4)]
            hi = [(P, [[(2 * b, LO, NT, 0), (2 * b + 1, LO, NT, 64)] for b in (2 * g, 2 * g + 1)]) for g in range(2)]
            self.groups = lo + hi
        else:
            self.NH = 1
            self.groups = [(LO, [[(0, 0, LO, 0)]]), (NT - LO, [[(0, LO, NT, 0)]])]
        self.NG = len(self.groups)
        self.psc = [ps(f"psc{k}", [P, 2, NT]) for k in range(2)]
        self.pt = [ps(f"pt{k}", [P, 2, 256]) for k in range(2)]
        self.po = ps("po", [P, 512])
        self.ex = sb("ex", [P, 2, 2, NT])
        self.mx = sb("mx", [P, 2, 2])
        self.zs = sb("zs", [P, 2, 2])
        self.lo = sb("lo", [P, self.NH, NT])
        self.hi = sb("hi", [self.KHI, self.NH, NT])
        if top:
            self.m8 = sb("m8", [P, 2, 2, 16])
            self.left = sb("left", [P, 2, 2, NT])
        self.g = Round(c.nc, tag, self.NAMES, self.NG)
        self.o = Round(c.nc, tag + "o", ["pv"], 1)
        self.half = Round(c.nc, tag + "h", ["first"], 2)
        if top:
            self.t = Round(c.nc, tag + "t", ["a", "b", "c", "d", "neg"], 2 * self.NG)

    def close(self):
        self.g.close()
        self.o.close()
        self.half.close()
        if self.top:
            self.t.close()

    def pe(self, m, s, q, k, v_lo, v_hi, ready, po_free, step=3.0):
        pe, g, c = self.c.nc.tensor, self.g, self.c
        NG = self.NG

        def scores(n):
            rows, tiles = self.groups[n]
            pe.wait_ge(g["exp"], g.now(m, n) - 2)
            for a, tile in enumerate(tiles):
                if self.many and rows == P and a == 1:
                    last.then_inc(self.half["first"], 1)
                    pe.wait_ge(self.half["first"], m * 2 + (n - 4) + 1)
                for h, q0, q1, p0 in tile:
                    j = slice(32 * (h // 2), 32 * (h // 2) + 32) if self.many else slice(0, P)
                    last = pe.matmul(self.psc[n % 2][p0:p0 + q1 - q0, a, :], q(j, h % 2, slice(q0, q1)), k[j, :],
                                     start=True, stop=True)
            last.then_inc(g["score"], 1)

        def turn(n):
            rows, tiles = self.groups[n]
            pe.wait_ge(g["norm"], g.now(m, n))
            pe.wait_ge(g["kept"], g.now(m, n) - 2)
            if rows == 64:
                apart(c, pe)
            for a in range(len(tiles)):
                x = self.ex[0:rows, n % 2, a, :]
                pe.transpose(self.pt[n % 2][:, 0, a * rows:(a + 1) * rows], x[:, 0:P], c.ident[0:rows, 0:rows])
                last = pe.transpose(self.pt[n % 2][0:self.KHI, 1, a * rows:(a + 1) * rows], x[:, P:], c.ident[0:rows, 0:rows])
            last.then_inc(g["turned"], 1)
        yield 0
        for sem, value in ready:
            pe.wait_ge(sem, value)
        scores(0)
        yield 0.5
        scores(1)
        for n in range(NG):
            if n + 2 < NG:
                yield 2.2 + step * n
                scores(n + 2)
            yield 2.5 + step * n
            turn(n)
        yield 2.51 + step * NG
        pe.wait_ge(g["kept"], g.now(m, NG - 1))
        for sem, value in po_free:
            pe.wait_ge(sem, value)
        if self.many:
            for j in range(4):
                f = slice(32 * j, 32 * j + 32)
                k4 = 0
                for x in range(2):
                    for keys, v in ((self.lo, v_lo), (self.hi, v_hi)):
                        last = pe.matmul(self.po[f, 0:c.NT], v[:, x * P + 32 * j:x * P + 32 * j + 32], keys[:, 2 * j + x, :],
                                         start=(k4 == 0), stop=(k4 == 3))
                        k4 += 1
        else:
            pe.matmul(self.po[:, 0:c.NT], v_lo, self.lo[:, 0, :], start=True, stop=False)
            last = pe.matmul(self.po[:, 0:c.NT], v_hi, self.hi[:, 0, :], start=False, stop=True)
        last.then_inc(self.o["pv"], 1)

    def act(self, m, s, step=3.0):
        act, g = self.c.nc.scalar, self.g

        def weights(n):
            rows, tiles = self.groups[n]
            act.wait_ge(g["rz"], g.now(m, n))
            for a in range(len(tiles)):
                last = act.activation(self.ex[0:rows, n % 2, a, :], self.ex[0:rows, n % 2, a, :], ACT.Copy,
                                      scale=self.zs[0:rows, n % 2, a:a + 1])
            last.then_inc(g["norm"], 1)

        def late(n):
            yield 2.4 + step * n
            weights(n)
            yield 3 + step * n
            if n == 0:
                act.wait_ge(self.o["pv"], m)
            self.keep(m, n, lambda to, x: act.activation(to, x, ACT.Copy), act)
        for n, (rows, tiles) in enumerate(self.groups):
            if self.top and n > 1:
                yield from late(n - 2)
            yield 1.5 + 0.2 * n if n < 2 else 3.2 + step * (n - 2)
            act.wait_ge(g["mx"], g.now(m, n))
            act.wait_ge(g["turned"], g.now(m, n) - 2)
            if self.top:
                act.wait_ge(g["norm"], g.now(m, n) - 2)
            for a in range(len(tiles)):
                last = act.activation(self.ex[0:rows, n % 2, a, :], self.psc[n % 2][0:rows, a, :], ACT.Exp,
                                      bias=self.mx[0:rows, n % 2, a:a + 1],
                                      **({} if self.top else {"accum_out": self.zs[0:rows, n % 2, a:a + 1]}))
            last.then_inc(g["exp"], 1)
        if self.top:
            yield from late(self.NG - 2)
            yield from late(self.NG - 1)

    def keep(self, m, n, copy, eng):
        rows, tiles = self.groups[n]
        eng.wait_ge(self.g["turned"], self.g.now(m, n))
        for half, parts, to in ((0, P, self.lo), (1, self.KHI, self.hi)):
            src = self.pt[n % 2][0:parts, half, 0:rows * len(tiles)]
            h0, nh = tiles[0][0][0], sum(len(t) for t in tiles)
            q = slice(0, self.LO) if rows == self.LO else slice(self.LO, self.c.NT)
            last = copy(to[:, h0:h0 + nh, q], src.rearrange("p (h q) -> p h q", q=q.stop - q.start))
        last.then_inc(self.g["kept"], 1)

    def dve(self, m, s, step=3.0):
        dve, g = self.c.nc.vector, self.g
        LO = self.LO

        def largest(n):
            rows, tiles = self.groups[n]
            dve.wait_ge(g["score"], g.now(m, n))
            dve.wait_ge(g["exp"], g.now(m, n) - 2)
            w = len(tiles)
            if not self.top:
                dve.tensor_reduce(self.mx[0:rows, n % 2, 0:w], self.psc[n % 2][0:rows, 0:w, :], AX.X, ALU.max,
                                  negate=True).then_inc(g["mx"], 1)
                return
            t = self.t
            k = lambda a: m * (2 * self.NG) + 2 * n + a + 1
            B, E, L = self.psc[n % 2], self.m8, self.left
            apart(self.c, dve)
            for a in range(w):
                dve.max(E[0:rows, n % 2, a, 0:8], B[0:rows, a, :]).then_inc(t["a"], 1)
            for a in range(w):
                dve.wait_ge(t["a"], k(a))
                apart(self.c, dve)
                dve.match_replace(L[0:rows, n % 2, a, :], E[0:rows, n % 2, a, 0:8], B[0:rows, a, :], self.BIG).then_inc(t["b"], 1)
            dve.tensor_scalar(self.mx[0:rows, n % 2, 0:w], E[0:rows, n % 2, 0:w, 0], -1.0, None, ALU.mult).then_inc(g["mx"], 1)
            for a in range(w):
                dve.wait_ge(t["b"], k(a))
                apart(self.c, dve)
                dve.max(E[0:rows, n % 2, a, 8:16], L[0:rows, n % 2, a, :]).then_inc(t["c"], 1)
            for a in range(w):
                dve.wait_ge(t["c"], k(a))
                apart(self.c, dve)
                dve.match_replace(L[0:rows, n % 2, a, :], E[0:rows, n % 2, a, 8:16], L[0:rows, n % 2, a, :], self.BIG).then_inc(t["d"], 1)

        def scaled(n):
            rows, tiles = self.groups[n]
            w = len(tiles)
            x = self.ex[0:rows, n % 2, 0:w, :]
            dve.wait_ge(g["exp"], g.now(m, n))
            if self.top:
                dve.wait_ge(self.t["d"], m * (2 * self.NG) + 2 * n + w)
                for a in range(w):
                    last = dve.scalar_tensor_tensor(self.ex[0:rows, n % 2, a, :], self.left[0:rows, n % 2, a, :], self.BIG,
                                                    self.ex[0:rows, n % 2, a, :], ALU.is_equal, ALU.mult,
                                                    accum_out=self.zs[0:rows, n % 2, a:a + 1])
                last.then_inc(g["z"], 1)
                dve.wait_ge(g["z"], g.now(m, n))
            dve.reciprocal(self.zs[0:rows, n % 2, 0:w], self.zs[0:rows, n % 2, 0:w]).then_inc(g["rz"], 1)
            if self.top:
                return
            dve.wait_ge(g["rz"], g.now(m, n))
            for a in range(w):
                last = dve.tensor_scalar(self.ex[0:rows, n % 2, a, :], self.ex[0:rows, n % 2, a, :],
                                         self.zs[0:rows, n % 2, a:a + 1], None, ALU.mult)
            last.then_inc(g["norm"], 1)

        yield 1
        largest(0)
        yield 1.2
        if self.NG > 1:
            largest(1)
        for n in range(self.NG):
            yield 2 + step * n
            scaled(n)
            if n + 2 < self.NG:
                yield 2.6 + step * n
                largest(n + 2)
            if not self.top:
                yield 3.1 + step * n
                if n == 0:
                    dve.wait_ge(self.o["pv"], m)
                self.keep(m, n, dve.tensor_copy, dve)


def attention_stage(c):
    nc, NT, N = c.nc, c.NT, c.N
    F4 = 4
    ctx = ExitStack()
    with ctx:
        sb = lambda n, s, d=F32: ctx.enter_context(nc.sbuf_tensor("att_" + n, s, d))
        ps = lambda n, s: ctx.enter_context(nc.psum_tensor("att_" + n, s, F32))
        names = ["x1", "qk", "k", "q", "v", "vkept", "resid", "x1b", "mob", "at", "wo", "r", "gate", "ge", "ge1", "gl",
                 "g", "diff", "x2", "x22", "gd", "x3", "f1", "gelu", "f2", "x4", "hs", "w_done"]
        r = Round(nc, "att", names + Norm.names("n2", "na", "n3", "nz"), 1, dma=["mo0", "mo1", "w"])
        wq, wk, wv, wo = (sb(n, [P, P]) for n in ("wq", "wk", "wv", "wo"))
        w1, w2, wg = sb("w1", [P, F4 * P]), sb("w2", [P, F4, P]), sb("wg", [P, 2, P])
        qmask = sb("qmask", [P, 2])
        bo = sb("bo", [P, 1])
        mo, x1, xn = sb("mo", [P, 2, NT]), sb("x1", [P, 2, NT]), sb("xn", [P, 2, NT])
        qeo, kk = sb("qeo", [P, 2, 2, NT]), sb("kk", [P, 2, NT])
        vlo, vhi = sb("vlo", [P, 2, 288]), sb("vhi", [P, 2, 288])
        resid, x1b, mob = sb("resid", [P, 2, NT]), sb("x1b", [P, 2, NT]), sb("mob", [P, 2, NT])
        at = sb("at", [P, 2, NT])
        rr, ao, gg, dd, x2, x3, xn3, x4 = (sb(n, [P, NT]) for n in ("rr", "ao", "gg", "dd", "x2", "x3", "xn3", "x4"))
        act1 = sb("act1", [P, F4, NT])
        pp = ps("pp", [P, 512])
        fa, fb = ps("fa", [P, 2, 256]), ps("fb", [P, 2, 256])
        faf = fa[:, :, :].rearrange("p a b -> p (a b)")
        heads_ = Heads(c, ctx, "atth", True, False)
        n2 = Norm(c, r, ctx, "n2", pp, c.eps[:, 0:1], c.col("n2g"), c.col("n2b"))
        na = Norm(c, r, ctx, "na", faf, c.eps[:, 0:1], c.col("ang"), c.col("anb"))
        fbf = fb[:, :, :].rearrange("p a b -> p (a b)")
        n3 = Norm(c, r, ctx, "n3", fbf, c.eps[:, 0:1], c.col("n3g"), c.col("n3b"))
        nz = Norm(c, r, ctx, "nz", fbf, c.eps[:, 0:1])
        H = lambda m: c.H[:, bass.ds(m * NT - NT, NT)]
        head_masks(c, "att", qmask, 0.25, (vlo, vhi))
        with nc.Block() as block:
            @block.sync
            def _(sp):
                for k, (t, n) in enumerate(((wq[:, :], "wq"), (wk[:, :], "wk"), (wv[:, :], "wv"), (wo[:, :], "wo"),
                                            (w1[:, :], "w1"), (w2[:, :, :], "w2"), (wg[:, :, :], "wg"))):
                    sp.dma_start(t, c.dram[n]).then_inc(r["w"], 16)
                    sp.wait_ge(r["w"], 32 + 16 * k)
        with nc.Block() as block:
            @block.tensor
            def _(pe):
                nc.tensor.matmul(pp[:, 0:1], wo[:, :], c.col("wv_b"), start=True, stop=True).then_inc(r["w_done"], 1)

            @block.vector
            def _(dve):
                dve.wait_ge(r["w_done"], 2)
                nc.vector.tensor_tensor(bo[:, :], pp[:, 0:1], c.col("wo_b"), ALU.add)
        STEP = 3.07
        with nc.Block() as block:
            @block.sync
            def _(sp):
                for m in (1, 2):
                    sp.dma_start(mo[:, m % 2, :], c.mo_dram[:, (m - 1) * NT:m * NT]).then_inc(r[f"mo{m % 2}"], 16)
                with sp.Fori(3, N, 2) as m:
                    for k, s in ((0, 1), (1, 0)):
                        at_, used = sp.snap((m + k - 1) * NT), sp.snap(m + (k - 1))
                        sp.wait_ge(r["mob"], used)
                        sp.dma_start(mo[:, s, :], c.mo_dram[:, bass.ds(at_, NT)]).then_inc(r[f"mo{s}"], 16)

            @block.gpsimd
            def _(pool):
                def prepare(m, s):
                    yield 0
                    pool.wait_ge(r[f"mo{s}"], m * 8 + (24 if s else 16))
                    old(pool, r["x1b"], m - 1)
                    nc.gpsimd.tensor_tensor(x1[:, s, :], H(m), mo[:, s, :], ALU.add).then_inc(r["x1"], 1)
                    yield from n2.pool(m, 0.7)

                def heads(m, s):
                    yield 1
                    pool.wait_ge(r["n2_out"], m + 1)
                    old(pool, r["r"], m - 1)
                    old(pool, r["x22"], m - 1)
                    old(pool, r["gate"], m - 1)
                    nc.gpsimd.tensor_tensor(resid[:, s, :], xn[:, s, :], bo[:, :].to_broadcast([P, NT]), ALU.add).then_inc(r["resid"], 1)
                    nc.gpsimd.tensor_copy(x1b[:, s, :], x1[:, s, :]).then_inc(r["x1b"], 1)
                    nc.gpsimd.tensor_copy(mob[:, s, :], mo[:, s, :]).then_inc(r["mob"], 1)

                def finish(m, s):
                    yield from na.pool(m, 1.1)
                    yield 9.5
                    pool.wait_ge(r["na_out"], m + 1)
                    pool.wait_ge(r["mob"], m + 1)
                    pool.wait_ge(r["x1b"], m + 1)
                    nc.gpsimd.tensor_tensor(dd[:, :], mob[:, s, :], ao[:, :], ALU.subtract).then_inc(r["diff"], 1)
                    nc.gpsimd.tensor_tensor(x2[:, :], x1b[:, s, :], ao[:, :], ALU.add).then_inc(r["x2"], 1)
                    yield 10.5
                    pool.wait_ge(r["x2"], m + 1)
                    nc.gpsimd.tensor_tensor(x2[:, :], x2[:, :], ao[:, :], ALU.add).then_inc(r["x22"], 1)
                    yield 16
                    pool.wait_ge(r["g"], m + 1)
                    pool.wait_ge(r["diff"], m + 1)
                    nc.gpsimd.tensor_tensor(dd[:, :], dd[:, :], gg[:, :], ALU.mult).then_inc(r["gd"], 1)
                    yield 18.5
                    pool.wait_ge(r["gd"], m + 1)
                    pool.wait_ge(r["x22"], m + 1)
                    pool.wait_ge(r["x4"], m)
                    nc.gpsimd.tensor_tensor(x3[:, :], x2[:, :], dd[:, :], ALU.add).then_inc(r["x3"], 1)

                def mlp(m, s):
                    yield from n3.pool(m, 0.89)
                    yield 18
                    pool.wait_ge(r["x4"], m + 1)
                    nc.gpsimd.tensor_tensor(x4[:, :], x4[:, :], H(m), ALU.add).then_inc(r["hs"], 1)
                    yield from nz.pool(m, 20)
                drive_four(c, pool, prepare, heads, finish, mlp)

            @block.tensor
            def _(pe):
                def prepare(m, s):
                    yield from n2.pe(m, 0.7, x1[:, s, :], [(r["x1"], m + 1), (r["vkept"], m)])
                    yield 13.4
                    pe.wait_ge(r["n2_out"], m + 1)
                    nc.tensor.matmul(pp[:, 0:NT], wq[:, :], xn[:, s, :], start=True, stop=True)
                    nc.tensor.matmul(pp[:, 256:256 + NT], wk[:, :], xn[:, s, :], start=True, stop=True).then_inc(r["qk"], 1)
                    yield 17
                    pe.wait_ge(r["q"], m + 1)
                    nc.tensor.matmul(pp[:, 0:P], xn[:, s, 0:P], wv[:, :], start=True, stop=True)
                    nc.tensor.matmul(pp[0:NT - P, P:2 * P], xn[:, s, P:], wv[:, :], start=True, stop=True).then_inc(r["v"], 1)

                def heads(m, s):
                    yield from heads_.pe(m, s, lambda j, x, rows: qeo[j, s, x, rows], kk[:, s, :], vlo[:, s, :],
                                         vhi[0:NT - P, s, :], [(r["q"], m + 1), (r["vkept"], m + 1)], [(r["at"], m)], STEP)

                def finish(m, s):
                    yield 0
                    pe.wait_ge(r["at"], m + 1)
                    pe.wait_ge(r["ge1"], m)
                    old(pe, r["gelu"], m - 1)
                    nc.tensor.matmul(fa[:, 0, 0:NT], wo[:, :], at[:, s, :], start=True, stop=True).then_inc(r["wo"], 1)
                    yield from na.pe(m, 1.1, rr[:, :], [(r["r"], m + 1)])
                    yield 9
                    pe.wait_ge(r["na_out"], m + 1)
                    pe.wait_ge(r["mob"], m + 1)
                    nc.tensor.matmul(fa[:, 0, 0:NT], wg[:, 0, :], mob[:, s, :], start=True, stop=False)
                    nc.tensor.matmul(fa[:, 0, 0:NT], wg[:, 1, :], ao[:, :], start=False, stop=True).then_inc(r["gate"], 1)

                def mlp(m, s):
                    yield from n3.pe(m, 0.89, x3[:, :], [(r["x3"], m + 1), (r["nz_lnv"], m)])
                    yield 14.5
                    pe.wait_ge(r["n3_out"], m + 1)
                    if not (isinstance(m, int) and m == N):
                        pe.wait_ge(r["ge1"], m + 2)
                    for k in range(F4):
                        last = nc.tensor.matmul((fa, fb)[k // 2][:, k % 2, 0:NT], w1[:, k * P:(k + 1) * P], xn3[:, :], start=True, stop=True)
                    last.then_inc(r["f1"], 1)
                    yield 16.5
                    pe.wait_ge(r["gelu"], m + 1)
                    for k in range(F4):
                        last = nc.tensor.matmul(fb[:, 0, 0:NT], w2[:, k, :], act1[:, k, :], start=(k == 0), stop=(k == F4 - 1))
                    last.then_inc(r["f2"], 1)
                    yield from nz.pe(m, 20, x4[:, :], [(r["hs"], m + 1)])
                drive_four(c, pe, prepare, heads, finish, mlp)

            @block.scalar
            def _(act):
                def prepare(m, s):
                    yield from n2.act(m, 0.7, xn[:, s, :], [(r["resid"], m - 1)] if old(None, None, m - 1) else [])
                    yield 14.4
                    act.wait_ge(r["qk"], m + 1)
                    old(act, heads_.g["score"], (m - 1) * heads_.NG)
                    nc.scalar.activation(kk[:, s, :], pp[:, 256:256 + NT], ACT.Identity, bias=c.col("wk_b")).then_inc(r["k"], 1)
                    yield 18
                    act.wait_ge(r["v"], m + 1)
                    old(act, heads_.o["pv"], m - 1)
                    for rows, v, at_ in ((P, vlo, 0), (NT - P, vhi, P)):
                        dst = v[0:rows, s, :].rearrange("p (x y) -> p x y", y=144)[:, :, 0:P]
                        dst = dst.rearrange("p x (j d) -> p x j d", d=32)[:, :, :, 0:16]
                        src = pp[0:rows, at_:at_ + P].rearrange("p (j x d) -> p x j d", x=2, d=16)
                        last = nc.scalar.activation(dst, src, ACT.Copy)
                    last.then_inc(r["vkept"], 1)

                def heads(m, s):
                    yield from heads_.act(m, s, STEP)
                    yield 2.5 + STEP * heads_.NG
                    act.wait_ge(heads_.o["pv"], m + 1)
                    old(act, r["wo"], m - 1)
                    nc.scalar.activation(at[:, s, :], heads_.po[:, 0:NT], ACT.Copy).then_inc(r["at"], 1)

                def finish(m, s):
                    yield from na.act(m, 1.1, ao[:, :], [(r["gate"], m), (r["x22"], m)])
                    yield 11
                    act.wait_ge(r["ge1"], m + 1)
                    nc.scalar.activation(gg[:, :], gg[:, :], ACT.Exp, scale=-1.0).then_inc(r["ge"], 1)
                    act.wait_ge(r["ge"], m + 1)
                    nc.scalar.activation(gg[:, :], gg[:, :], ACT.Ln, bias=c.eps[:, 3:4]).then_inc(r["gl"], 1)
                    act.wait_ge(r["gl"], m + 1)
                    nc.scalar.activation(gg[:, :], gg[:, :], ACT.Exp, scale=-1.0).then_inc(r["g"], 1)

                def mlp(m, s):
                    yield from n3.act(m, 0.89, xn3[:, :], [(r["f1"], m)])
                    yield 15.5
                    act.wait_ge(r["f1"], m + 1)
                    act.wait_ge(r["f2"], m)
                    for k in range(F4):
                        last = nc.scalar.activation(act1[:, k, :], (fa, fb)[k // 2][:, k % 2, 0:NT], ACT.Gelu_apprx_tanh, bias=c.col("f_b1", k))
                    last.then_inc(r["gelu"], 1)
                    nc.scalar.preload_act_table_set(LN_SETS)
                    yield from nz.act(m, 20)
                nc.scalar.preload_act_table_set(LN_SETS)
                drive_four(c, act, prepare, heads, finish, mlp)

            @block.vector
            def _(dve):
                def prepare(m, s):
                    yield from n2.dve(m, 0.7, x1[:, s, :])
                    yield 15
                    dve.wait_ge(r["k"], m + 1)
                    old(dve, heads_.g["score"], (m - 1) * heads_.NG)
                    for x in range(2):
                        last = nc.vector.tensor_scalar(qeo[:, s, x, :], pp[:, 0:NT], c.col("wq_b"), qmask[:, x:x + 1], ALU.add, ALU.mult)
                    last.then_inc(r["q"], 1)

                def heads(m, s):
                    yield from heads_.dve(m, s, STEP)

                def finish(m, s):
                    yield 1
                    dve.wait_ge(r["wo"], m + 1)
                    dve.wait_ge(r["resid"], m + 1)
                    nc.vector.tensor_tensor(rr[:, :], fa[:, 0, 0:NT], resid[:, s, :], ALU.add).then_inc(r["r"], 1)
                    yield 1.5
                    dve.wait_ge(r["r"], m + 1)
                    yield from na.dve(m, 1.1, rr[:, :])
                    yield 10
                    dve.wait_ge(r["gate"], m + 1)
                    dve.wait_ge(r["gd"], m)
                    nc.vector.tensor_scalar(gg[:, :], fa[:, 0, 0:NT], c.col("gate_b"), c.LOW, ALU.add, ALU.max).then_inc(r["ge1"], 1)

                def mlp(m, s):
                    yield from n3.dve(m, 0.89, x3[:, :])
                    yield 17.5
                    dve.wait_ge(r["f2"], m + 1)
                    nc.vector.scalar_tensor_tensor(x4[:, :], fb[:, 0, 0:NT], c.col("f_b2"), x3[:, :], ALU.add, ALU.add).then_inc(r["x4"], 1)
                    yield from nz.dve(m, 20, x4[:, :], out=H(m))
                drive_four(c, dve, prepare, heads, finish, mlp)
        heads_.close()
        r.close()


def top_attention_stage(c):
    nc, NT, N = c.nc, c.NT, c.N
    ctx = ExitStack()
    with ctx:
        sb = lambda n, s, d=F32: ctx.enter_context(nc.sbuf_tensor("top_" + n, s, d))
        ps = lambda n, s: ctx.enter_context(nc.psum_tensor("top_" + n, s, F32))
        names = ["p0", "p1", "xp", "qk", "k", "q", "v", "vkept", "at", "wo", "r", "w_done"]
        r = Round(nc, "top", names + Norm.names("tz"), 1, dma=["w"])
        wqkv, wo = sb("wqkv", [P, 3 * P]), sb("wo", [P, P])
        qmask, bo, w1p = sb("qmask", [P, 2]), sb("bo", [P, 1]), sb("w1p", [P, 1])
        xp = sb("xp", [P, NT])
        qeo, kk = sb("qeo", [P, 2, 2, NT]), sb("kk", [P, 2, NT])
        vlo, vhi = sb("vlo", [P, 2, 288]), sb("vhi", [P, 2, 288])
        at, rr = sb("at", [P, 2, NT]), sb("rr", [P, NT])
        pp, fa = ps("pp", [P, 512]), ps("fa", [P, 512])
        heads_ = Heads(c, ctx, "toph", True, True)
        nz = Norm(c, r, ctx, "tz", fa, c.eps[:, 0:1])
        H = lambda m: c.H[:, bass.ds(m * NT - NT, NT)]
        head_masks(c, "top", qmask, float(P) ** -0.5, (vlo, vhi))
        with nc.Block() as block:
            @block.sync
            def _(sp):
                for k, (t, n) in enumerate(((wqkv[:, :], "qkv"), (wo[:, :], "wo2"))):
                    sp.dma_start(t, c.dram[n]).then_inc(r["w"], 16)
                    sp.wait_ge(r["w"], 32 + 16 * k)
        with nc.Block() as block:
            @block.tensor
            def _(pe):
                nc.tensor.matmul(pp[:, 0:1], wo[:, :], c.col("v2_b"), start=True, stop=True).then_inc(r["w_done"], 1)

            @block.vector
            def _(dve):
                nc.vector.tensor_scalar(w1p[:, :], c.col("pos_w", 1), 1.0, None, ALU.add)
                dve.wait_ge(r["w_done"], 2)
                nc.vector.tensor_tensor(bo[:, :], pp[:, 0:1], c.col("o2_b"), ALU.add)
        STEP = 3.6
        with nc.Block() as block:
            @block.gpsimd
            def _(pool):
                def prepare(m, s):
                    yield 0

                def heads(m, s):
                    yield 0

                def finish(m, s):
                    yield from nz.pool(m, 4.99)
                drive(c, pool, prepare, heads, finish)

            @block.tensor
            def _(pe):
                def prepare(m, s):
                    yield 1.21
                    pe.wait_ge(r["xp"], m + 1)
                    pe.wait_ge(r["vkept"], m)
                    nc.tensor.matmul(pp[:, 0:NT], wqkv[:, 0:P], xp[:, :], start=True, stop=True)
                    nc.tensor.matmul(pp[:, 256:256 + NT], wqkv[:, P:2 * P], xp[:, :], start=True, stop=True).then_inc(r["qk"], 1)
                    yield 6
                    pe.wait_ge(r["q"], m + 1)
                    nc.tensor.matmul(pp[:, 0:P], xp[:, 0:P], wqkv[:, 2 * P:], start=True, stop=True)
                    nc.tensor.matmul(pp[0:NT - P, P:2 * P], xp[:, P:], wqkv[:, 2 * P:], start=True, stop=True).then_inc(r["v"], 1)

                def heads(m, s):
                    yield from heads_.pe(m, s, lambda j, x, rows: qeo[j, s, x, rows], kk[:, s, :], vlo[:, s, :],
                                         vhi[0:NT - P, s, :], [(r["q"], m + 1), (r["vkept"], m + 1)], [(r["at"], m)], STEP)

                def finish(m, s):
                    yield 0
                    pe.wait_ge(r["at"], m + 1)
                    pe.wait_ge(r["tz_lnv"], m)
                    nc.tensor.matmul(fa[:, 0:NT], wo[:, :], at[:, s, :], start=True, stop=True).then_inc(r["wo"], 1)
                    yield from nz.pe(m, 4.99, rr[:, :], [(r["r"], m + 1)])
                drive(c, pe, prepare, heads, finish)

            @block.scalar
            def _(act):
                def prepare(m, s):
                    yield 2
                    act.wait_ge(r["qk"], m + 1)
                    old(act, heads_.g["score"], (m - 1) * heads_.NG)
                    nc.scalar.activation(kk[:, s, :], pp[:, 256:256 + NT], ACT.Identity, bias=c.col("k2_b")).then_inc(r["k"], 1)
                    yield 10
                    act.wait_ge(r["v"], m + 1)
                    old(act, heads_.o["pv"], m - 1)
                    for rows, v, at_ in ((P, vlo, 0), (NT - P, vhi, P)):
                        dst = v[0:rows, s, :].rearrange("p (x y) -> p x y", y=144)[:, :, 0:P]
                        dst = dst.rearrange("p x (j d) -> p x j d", d=32)[:, :, :, 0:16]
                        src = pp[0:rows, at_:at_ + P].rearrange("p (j x d) -> p x j d", x=2, d=16)
                        last = nc.scalar.activation(dst, src, ACT.Copy)
                    last.then_inc(r["vkept"], 1)

                def heads(m, s):
                    yield from heads_.act(m, s, STEP)
                    yield 2.5 + STEP * heads_.NG
                    act.wait_ge(heads_.o["pv"], m + 1)
                    old(act, r["wo"], m - 1)
                    nc.scalar.activation(at[:, s, :], heads_.po[:, 0:NT], ACT.Copy).then_inc(r["at"], 1)

                def finish(m, s):
                    yield from nz.act(m, 4.99)
                nc.scalar.preload_act_table_set(LN_SETS)
                drive(c, act, prepare, heads, finish)

            @block.vector
            def _(dve):
                def prepare(m, s):
                    yield 0
                    dve.wait_ge(r["v"], m)
                    nc.vector.tensor_scalar(xp[:, :], H(m), w1p[:, :], c.col("pos_b"), ALU.mult, ALU.add).then_inc(r["p0"], 1)
                    yield 0
                    dve.wait_ge(r["p0"], m + 1)
                    nc.vector.scalar_tensor_tensor(xp[:, 1:], c.H[:, bass.ds(m * NT - NT, NT - 1)], c.col("pos_w", 0), xp[:, 1:],
                                                   ALU.mult, ALU.add).then_inc(r["p1"], 1)
                    yield 1
                    dve.wait_ge(r["p1"], m + 1)
                    nc.vector.scalar_tensor_tensor(xp[:, 0:NT - 1], c.H[:, bass.ds(m * NT - NT + 1, NT - 1)], c.col("pos_w", 2),
                                                   xp[:, 0:NT - 1], ALU.mult, ALU.add).then_inc(r["xp"], 1)
                    yield 2.49
                    dve.wait_ge(r["k"], m + 1)
                    old(dve, heads_.g["score"], (m - 1) * heads_.NG)
                    for x in range(2):
                        last = nc.vector.tensor_scalar(qeo[:, s, x, :], pp[:, 0:NT], c.col("q2_b"), qmask[:, x:x + 1], ALU.add, ALU.mult)
                    last.then_inc(r["q"], 1)

                def heads(m, s):
                    yield from heads_.dve(m, s, STEP)

                def finish(m, s):
                    yield 1.82
                    dve.wait_ge(r["wo"], m + 1)
                    nc.vector.scalar_tensor_tensor(rr[:, :], fa[:, 0:NT], bo[:, :], H(m), ALU.add, ALU.add).then_inc(r["r"], 1)
                    dve.wait_ge(r["r"], m + 1)
                    yield from nz.dve(m, 4.99, rr[:, :], out=H(m))
                drive(c, dve, prepare, heads, finish)
        heads_.close()
        r.close()


def relu_attention_stage(c):
    nc, NT, N = c.nc, c.NT, c.N
    SCALE = 0.25
    ctx = ExitStack()
    with ctx:
        sb = lambda n, s, d=F32: ctx.enter_context(nc.sbuf_tensor("rel_" + n, s, d))
        ps = lambda n, s: ctx.enter_context(nc.psum_tensor("rel_" + n, s, F32))
        names = ["hc", "qk", "qkept", "v", "vb", "vkept", "at", "wo", "r", "hs"]
        r = Round(nc, "rel", names + Norm.names("ra", "rz"), 1, dma=["w"])
        w = sb("w", [P, 4, P])
        bvb, bq = sb("bvb", [P, P]), sb("bq", [P, 1])
        hc = sb("hc", [P, NT])
        qk = sb("qk", [P, 2, 2, NT])
        v = sb("v", [P, 2, 2, P])
        at, rr, ao, hs = sb("at", [P, 2, NT]), sb("rr", [P, NT]), sb("ao", [P, NT]), sb("hs", [P, NT])
        pp, fa = ps("pp", [P, 512]), ps("fa", [P, 512])
        heads_ = Heads(c, ctx, "relh", False, False)
        ra = Norm(c, r, ctx, "ra", fa, c.eps[:, 2:3], c.col("g3"), c.col("b3"))
        rz = Norm(c, r, ctx, "rz", fa, c.eps[:, 0:1])
        H = lambda m: c.H[:, bass.ds(m * NT - NT, NT)]
        with nc.Block() as block:
            @block.sync
            def _(sp):
                for k, (t, n) in enumerate((*((w[:, q, :], "w3" + "qkvo"[q]) for q in range(4)), (bvb[:, :], "bv3"))):
                    sp.dma_start(t, c.dram[n]).then_inc(r["w"], 16)
                    sp.wait_ge(r["w"], 32 + 16 * k)
        with nc.Block() as block:
            @block.vector
            def _(dve):
                nc.vector.tensor_scalar(bq[:, :], c.col("q3_b"), SCALE, None, ALU.mult)
        STEP = 3.2
        with nc.Block() as block:
            @block.gpsimd
            def _(pool):
                def prepare(m, s):
                    yield 0
                    pool.wait_ge(r["v"], m)
                    nc.gpsimd.tensor_copy(hc[:, :], H(m)).then_inc(r["hc"], 1)

                def heads(m, s):
                    yield 1.18

                def finish(m, s):
                    yield from ra.pool(m, 0.86)
                    yield 6
                    pool.wait_ge(r["ra_out"], m + 1)
                    pool.wait_ge(r["rz_xc"], m)
                    nc.gpsimd.tensor_tensor(hs[:, :], H(m), ao[:, :], ALU.add).then_inc(r["hs"], 1)
                    yield from rz.pool(m, 7)
                drive(c, pool, prepare, heads, finish)

            @block.tensor
            def _(pe):
                def prepare(m, s):
                    yield 1.36
                    pe.wait_ge(r["vb"], m)
                    for q in range(2):
                        last = nc.tensor.matmul(pp[:, q * 256:q * 256 + NT], w[:, q, :], H(m), start=True, stop=True)
                    last.then_inc(r["qk"], 1)
                    yield 8.4
                    pe.wait_ge(r["qkept"], m + 1)
                    pe.wait_ge(r["hc"], m + 1)
                    nc.tensor.matmul(pp[:, 0:P], hc[:, 0:P], w[:, 2, :], start=True, stop=True)
                    nc.tensor.matmul(pp[0:NT - P, P:2 * P], hc[:, P:], w[:, 2, :], start=True, stop=True).then_inc(r["v"], 1)

                def heads(m, s):
                    yield from heads_.pe(m, s, lambda j, x, rows: qk[j, s, 0, rows], qk[:, s, 1, :], v[:, s, 0, :],
                                         v[0:NT - P, s, 1, :], [(r["qkept"], m + 1), (r["vkept"], m + 1)], [(r["at"], m)], STEP)

                def finish(m, s):
                    yield 0
                    pe.wait_ge(r["at"], m + 1)
                    pe.wait_ge(r["rz_lnv"], m)
                    nc.tensor.matmul(fa[:, 0:NT], w[:, 3, :], at[:, s, :], start=True, stop=True).then_inc(r["wo"], 1)
                    yield from ra.pe(m, 0.86, rr[:, :], [(r["r"], m + 1)])
                    yield from rz.pe(m, 7, hs[:, :], [(r["hs"], m + 1)])
                drive(c, pe, prepare, heads, finish)

            @block.scalar
            def _(act):
                def prepare(m, s):
                    yield 3.8
                    act.wait_ge(r["qk"], m + 1)
                    old(act, heads_.g["score"], (m - 1) * heads_.NG)
                    nc.scalar.activation(qk[:, s, 0, :], pp[:, 0:NT], ACT.Relu, scale=SCALE, bias=bq[:, :])
                    nc.scalar.activation(qk[:, s, 1, :], pp[:, 256:256 + NT], ACT.Relu, bias=c.col("k3_b")).then_inc(r["qkept"], 1)

                def heads(m, s):
                    yield from heads_.act(m, s, STEP)
                    yield 2.5 + STEP * heads_.NG
                    act.wait_ge(heads_.o["pv"], m + 1)
                    old(act, r["wo"], m - 1)
                    nc.scalar.activation(at[:, s, :], heads_.po[:, 0:NT], ACT.Copy).then_inc(r["at"], 1)

                def finish(m, s):
                    yield 0
                    act.wait_ge(r["wo"], m + 1)
                    act.wait_ge(r["ra_xc"], m)
                    nc.scalar.activation(rr[:, :], fa[:, 0:NT], ACT.Relu, bias=c.col("o3_b")).then_inc(r["r"], 1)
                    yield from ra.act(m, 0.86, ao[:, :], [(r["hs"], m)])
                    yield from rz.act(m, 7)
                nc.scalar.preload_act_table_set(LN_SETS)
                drive(c, act, prepare, heads, finish)

            @block.vector
            def _(dve):
                def prepare(m, s):
                    yield 9.4
                    dve.wait_ge(r["v"], m + 1)
                    old(dve, heads_.o["pv"], m - 1)
                    nc.vector.tensor_tensor(v[:, s, 0, :], pp[:, 0:P], bvb[:, :], ALU.add)
                    nc.vector.tensor_tensor(v[0:NT - P, s, 1, :], pp[0:NT - P, P:2 * P], bvb[0:NT - P, :], ALU.add).then_inc(r["vb"], 1)
                    dve.wait_ge(r["vb"], m + 1)
                    nc.vector.tensor_scalar(v[:, s, 0, :], v[:, s, 0, :], 0.0, None, ALU.max)
                    nc.vector.tensor_scalar(v[0:NT - P, s, 1, :], v[0:NT - P, s, 1, :], 0.0, None, ALU.max).then_inc(r["vkept"], 1)

                def heads(m, s):
                    yield from heads_.dve(m, s, STEP)

                def finish(m, s):
                    yield from ra.dve(m, 0.86, rr[:, :])
                    yield from rz.dve(m, 7, hs[:, :], out=H(m))
                drive(c, dve, prepare, heads, finish)
        heads_.close()
        r.close()


def experts_stage(c, out):
    nc, NT, N, T, G = c.nc, c.NT, c.N, c.T, c.G
    E, F4 = 16, 4
    CAP = expert_capacity(T, E)
    ROW = P + E
    JB = P // E
    NB = -(-NT // JB)
    TILES = -(-CAP // P)
    LOW, HIGH = P // 2, 2 * TILES
    table, acc = c.dram["table"], c.dram["acc"]
    trow = table[0:T, :].rearrange("(b j) d -> b j d", j=NT)
    arow = acc[0:T, :].rearrange("(b j) d -> b j d", j=NT)
    PADS = table.shape[0] - T
    ctx = ExitStack()
    with ctx:
        sb = lambda n, s, d=F32: ctx.enter_context(nc.sbuf_tensor("moe_" + n, s, d))
        slots = sb("idx", [P, E * TILES], U32)
        with ExitStack() as own:
            sbo = lambda n, s, d=F32: own.enter_context(nc.sbuf_tensor("gat_" + n, s, d))
            probs = sbo("probs", [N, NT, E])
            gate_tokens(c, probs, trow, arow, E, F4, PADS)
            choose_slots(c, probs, slots, E, CAP, JB, NB, LOW, HIGH, TILES)
        run_experts(c, slots, E, F4, TILES, ROW)
        last_norm(c, arow, out)


def expert_capacity(tokens, experts):
    groups = -(-tokens // 1024)
    while tokens % groups or groups % experts:
        groups += 1
    return max(int(round(1.0 * (tokens // groups) * groups / experts)), 8)


def gate_tokens(c, probs, trow, arow, E, F4, PADS):
    nc, NT, N, G = c.nc, c.NT, c.N, c.G
    ctx = ExitStack()
    with ctx:
        sb = lambda n, s, d=F32: ctx.enter_context(nc.sbuf_tensor("gt_" + n, s, d))
        ps = lambda n, s: ctx.enter_context(nc.psum_tensor("gt_" + n, s, F32))
        r = Round(nc, "gtk", ["hj", "logit", "f1", "gelu", "f2", "turned", "row", "sum"], G)
        w = Round(nc, "gtw", ["max", "sub", "exp", "sums", "rec", "probs", "prow", "zero", "biased"], 1, dma=["w", "row_out", "acc_out", "pad"])
        sw1, sw2, wgate = sb("sw1", [P, F4 * P]), sb("sw2", [P, F4, P]), sb("wgate", [P, E])
        b2 = sb("b2", [N, P])
        zero = sb("zero", [PADS, P + E])
        hj = sb("hj", [P, 2, N])
        hid = sb("hid", [P, 2, F4, N])
        rows = sb("rows", [N, G, P + E])
        accs = sb("accs", [N, G, P])
        lg, mx, sm = sb("lg", [N, G, E]), sb("mx", [N, G]), sb("sm", [N, G])
        pl = ps("pl", [N, G, E])
        pt = [ps(f"pt{k}", [N, P]) for k in range(2)]
        pf = [ps(f"pf{k}", [P, F4, N]) for k in range(2)]
        po = [ps(f"po{k}", [N, P]) for k in range(2)]
        Hj = c.H[:, :].rearrange("p (b t) -> p b t", t=NT)
        prev = lambda i, k: r.now(i, k) - (1 if k == 0 else 2)
        with nc.Block() as block:
            @block.sync
            def _(sp):
                for k, (t, s) in enumerate(((sw1[:, :], "sw1"), (sw2[:, :, :], "sw2"), (wgate[:, :], "wgate"))):
                    sp.dma_start(t, c.dram[s]).then_inc(w["w"], 16)
                    sp.wait_ge(w["w"], 32 + 16 * k)
                sp.dma_start(b2[:, :], c.dram["sb2b"][0:N, :]).then_inc(w["w"], 16)
                sp.wait_ge(w["w"], 80)

            @block.gpsimd
            def _(pool):
                nc.gpsimd.memset(zero[:, :], 0.0).then_inc(w["zero"], 1)
        with nc.Block() as block:
            @block.sync
            def _(sp):
                sp.dma_start(c.dram["table"][c.T:, :], zero[:, :]).then_inc(w["pad"], 16)
                sp.dma_start(c.dram["acc"][c.T:, :], zero[:, 0:P]).then_inc(w["pad"], 16)
                with sp.Fori(1, G + 1) as i:
                    at = sp.snap(i * G - G)
                    sp.wait_ge(w["prow"], i + 1)
                    sp.dma_start(trow[:, bass.ds(at, G), :], rows[:, :, :]).then_inc(w["row_out"], 16)
                    sp.wait_ge(w["biased"], i + 1)
                    sp.dma_start(arow[:, bass.ds(at, G), :], accs[:, :, :]).then_inc(w["acc_out"], 16)
                sp.wait_ge(w["pad"], 48)
                sp.wait_ge(w["row_out"], loaded(G))
                sp.wait_ge(w["acc_out"], loaded(G))

            @block.gpsimd
            def _(pool):
                with pool.Fori(1, G + 1) as i:
                    for k in range(G):
                        if k == 0:
                            pool.wait_ge(r["turned"], r.now(i, 0) - 1)
                        pool.wait_ge(r["f1"], prev(i, k))
                        pool.wait_ge(r["turned"], prev(i, k))
                        pool.wait_ge(r["logit"], prev(i, k))
                        nc.gpsimd.tensor_copy(hj[:, k % 2, :], Hj[:, :, bass.ds(i * G + (k - G), 1)].rearrange("p b o -> p (b o)")).then_inc(r["hj"], 1)

            @block.tensor
            def _(pe):
                def second(i, k):
                    s = k % 2
                    pe.wait_ge(r["gelu"], r.now(i, k))
                    pe.wait_ge(r["sum"], prev(i, k))
                    for q in range(F4):
                        last = nc.tensor.matmul(po[s][:, :], hid[:, s, q, :], sw2[:, q, :], start=(q == 0), stop=(q == F4 - 1))
                    last.then_inc(r["f2"], 1)
                with pe.Fori(1, G + 1) as i:
                    for k in range(G):
                        s = k % 2
                        pe.wait_ge(r["hj"], r.now(i, k))
                        if k == 0:
                            pe.wait_ge(w["sub"], i)
                            pe.wait_ge(w["max"], i)
                        nc.tensor.matmul(pl[:, k, :], hj[:, s, :], wgate[:, :], start=True, stop=True).then_inc(r["logit"], 1)
                        pe.wait_ge(r["row"], prev(i, k))
                        nc.tensor.transpose(pt[s][:, :], hj[:, s, :], c.ident[:, :]).then_inc(r["turned"], 1)
                        pe.wait_ge(r["gelu"], prev(i, k))
                        for q in range(F4):
                            last = nc.tensor.matmul(pf[s][:, q, :], sw1[:, q * P:(q + 1) * P], hj[:, s, :], start=True, stop=True)
                        last.then_inc(r["f1"], 1)
                        if k:
                            second(i, k - 1)
                    second(i, G - 1)

            @block.scalar
            def _(act):
                with act.Fori(1, G + 1) as i:
                    for k in range(G):
                        s = k % 2
                        act.wait_ge(r["f1"], r.now(i, k))
                        act.wait_ge(r["f2"], prev(i, k))
                        for q in range(F4):
                            last = nc.scalar.activation(hid[:, s, q, :], pf[s][:, q, :], ACT.Gelu_apprx_tanh, bias=c.col("sb1", q))
                        last.then_inc(r["gelu"], 1)
                    act.wait_ge(w["sub"], i + 1)
                    nc.scalar.activation(lg[:, :, :], lg[:, :, :], ACT.Exp).then_inc(w["exp"], 1)

            @block.vector
            def _(dve):
                def total(i, k):
                    dve.wait_ge(r["f2"], r.now(i, k))
                    dve.wait_ge(r["row"], r.now(i, k))
                    if k == 0:
                        dve.wait_ge(w["acc_out"], sent(i))
                    nc.vector.tensor_tensor(accs[:, k, :], po[k % 2][:, :], rows[:, k, 0:P], ALU.add).then_inc(r["sum"], 1)
                with dve.Fori(1, G + 1) as i:
                    for k in range(G):
                        s = k % 2
                        dve.wait_ge(r["turned"], r.now(i, k))
                        if k == 0:
                            dve.wait_ge(w["row_out"], sent(i))
                        nc.vector.tensor_copy(rows[:, k, 0:P], pt[s][:, :]).then_inc(r["row"], 1)
                        if k:
                            total(i, k - 1)
                    total(i, G - 1)
                    dve.wait_ge(r["logit"], r.now(i, G - 1))
                    nc.vector.tensor_reduce(mx[:, :], pl[:, :, :], AX.X, ALU.max).then_inc(w["max"], 1)
                    dve.wait_ge(w["max"], i + 1)
                    nc.vector.tensor_tensor(lg[:, :, :], pl[:, :, :], across(mx[:, :], 2, E), ALU.subtract).then_inc(w["sub"], 1)
                    dve.wait_ge(w["exp"], i + 1)
                    nc.vector.tensor_reduce(sm[:, :], lg[:, :, :], AX.X, ALU.add).then_inc(w["sums"], 1)
                    dve.wait_ge(w["sums"], i + 1)
                    nc.vector.reciprocal(sm[:, :], sm[:, :]).then_inc(w["rec"], 1)
                    dve.wait_ge(w["rec"], i + 1)
                    now = bass.ds(i * G - G, G)
                    nc.vector.tensor_tensor(probs[:, now, :], lg[:, :, :], across(sm[:, :], 2, E), ALU.mult).then_inc(w["probs"], 1)
                    nc.vector.tensor_tensor(rows[:, :, P:], lg[:, :, :], across(sm[:, :], 2, E), ALU.mult).then_inc(w["prow"], 1)
                    dve.wait_ge(r["sum"], r.now(i, G - 1))
                    nc.vector.tensor_tensor(accs[:, :, :], accs[:, :, :], across(b2[:, :], 1, G), ALU.add).then_inc(w["biased"], 1)
        r.close()
        w.close()


def choose_slots(c, probs, slots, E, CAP, JB, NB, LOW, HIGH, TILES):
    nc, NT, N, T, G = c.nc, c.NT, c.N, c.T, c.G
    VALUE_BITS, INDEX_BITS = 30, 15
    FAR = 1.0e6
    assert T <= 1 << INDEX_BITS
    TAIL = NT - (NB - 1) * JB
    BLK = 512 // N if N <= 128 else 4
    with ExitStack() as outer:
        sbo = lambda n, s, d=F32: outer.enter_context(nc.sbuf_tensor("ch_" + n, s, d))
        hi_b, lo_b = sbo("hi", [N, NT, E], BF16), sbo("lo", [N, NT, E], BF16)
        con = sbo("con", [P, 2 * P + 1 + TILES])
        comb = sbo("comb", [2 * HIGH, 2, TILES])
        with ExitStack() as ctx:
            sb = lambda n, s, d=F32: ctx.enter_context(nc.sbuf_tensor("cs_" + n, s, d))
            ps = lambda n, s: ctx.enter_context(nc.psum_tensor("cs_" + n, s, F32))
            key = sb("key", [P, NB, N])
            idx = sb("idx", [P, NB, N])
            sel = sb("sel", [P, NB, N])
            small = sb("small", [P, 8])
            bits = sb("bits", [P, 4], U32)
            pc = ps("pc", [P, 8])
            pk = [ps(f"pk{k}", [P, P]) for k in range(2)]
            r = Round(nc, "chs", ["step", "sum", "iota", "turn", "copy", "tb", "tc"], 1, dma=["c0", "c1"])
            cnt, tot, bitf, need, lim, cand, offs = (small[:, k:k + 1] for k in range(7))
            best, bit_u, cand_u, hit_u = (bits[:, k:k + 1] for k in range(4))
            group, prefix, pj = con[:, 0:P], con[:, P:2 * P], con[:, 2 * P:2 * P + 1]
            flat = lambda t: t[:, :, :].rearrange("p a b -> p (a b)")
            pf = probs[:, :, :].rearrange("b j e -> b (j e)")
            with nc.Block() as block:
                @block.sync
                def _(sp):
                    sp.dma_start(con[:, :], c.dram["con"]).then_inc(r["c0"], 16)
                    sp.dma_start(comb[:, :, :], c.dram["comb"]).then_inc(r["c1"], 16)
                    sp.wait_ge(r["c0"], 32)
                    sp.wait_ge(r["c1"], 32)

                @block.gpsimd
                def _(pool):
                    nc.gpsimd.iota(idx[:, :, :], [[JB, NB], [NT, N]], base=0, channel_multiplier=0,
                                   allow_small_or_imprecise_dtypes=True)

                @block.vector
                def _(dve):
                    nc.vector.memset(key[:, NB - 1, :], -1.0)

                @block.tensor
                def _(pe):
                    for k in range(NB):
                        w = min(P, NT * E - k * P)
                        if k >= 2:
                            pe.wait_ge(r["copy"], k)
                        nc.tensor.transpose(pk[k % 2][0:w, 0:N], pf[:, k * P:k * P + w], c.ident[0:N, 0:N]).then_inc(r["turn"], 1)

                @block.scalar
                def _(act):
                    for k in range(NB - 1):
                        act.wait_ge(r["turn"], k + 2)
                        nc.scalar.activation(key[:, k, :], pk[k % 2][:, 0:N], ACT.Copy).then_inc(r["copy"], 1)
            with nc.Block() as block:
                @block.scalar
                def _(act):
                    w = TAIL * E
                    nc.scalar.activation(key[0:w, NB - 1, :], pk[(NB - 1) % 2][0:w, 0:N], ACT.Copy).then_inc(r["copy"], 1)

                @block.vector
                def _(dve):
                    nc.vector.tensor_scalar(idx[:, :, :], idx[:, :, :], pj, None, ALU.add)
                    nc.vector.memset(bits[:, :], 0)
                    nc.vector.memset(small[:, :], 0.0)
            with nc.Block() as block:
                @block.vector
                def _(dve):
                    nc.vector.memset(bitf, float(1 << (VALUE_BITS - 1)))
            STEPS = 8
            rs = Round(nc, "chl", ["step"], STEPS)
            rt = Round(nc, "cht", ["step"], STEPS)
            with nc.Block() as block:
                @block.tensor
                def _(pe):
                    with pe.Fori(1, VALUE_BITS + 1) as i:
                        pe.wait_ge(rs["step"], i * STEPS + 3)
                        nc.tensor.matmul(pc[:, 0:1], group, cnt, start=True, stop=True).then_inc(r["sum"], 1)
                    pe.wait_ge(r["step"], 2)
                    nc.tensor.matmul(pc[:, 0:1], group, cnt, start=True, stop=True).then_inc(r["sum"], 1)
                    with pe.Fori(1, INDEX_BITS + 1) as i:
                        pe.wait_ge(rt["step"], i * STEPS + 2)
                        nc.tensor.matmul(pc[:, 0:1], group, cnt, start=True, stop=True).then_inc(r["tb"], 1)

                @block.vector
                def _(dve):
                    with dve.Fori(1, VALUE_BITS + 1) as i:
                        n = [0]

                        def step(ins):
                            n[0] += 1
                            ins.then_inc(rs["step"], 1)
                            dve.wait_ge(rs["step"], i * STEPS + n[0])
                        step(nc.vector.tensor_copy(bit_u, bitf))
                        step(nc.vector.tensor_tensor(cand_u, best, bit_u, ALU.bitwise_or))
                        step(nc.vector.tensor_scalar(flat(sel), flat(key), cand_u.bitcast(F32), None, ALU.is_ge, ALU.add, accum_out=cnt))
                        dve.wait_ge(r["sum"], i + 1)
                        step(nc.vector.tensor_scalar(hit_u, pc[:, 0:1], float(CAP), bitf, ALU.is_ge, ALU.mult))
                        step(nc.vector.tensor_tensor(best, best, hit_u, ALU.bitwise_or))
                        step(nc.vector.tensor_scalar(bitf, bitf, 0.5, None, ALU.mult))
                        while n[0] < STEPS:
                            n[0] += 1
                            dve.sem_inc(rs["step"], 1)
                    t = best.bitcast(F32)
                    k = [1]

                    def one(ins):
                        k[0] += 1
                        ins.then_inc(r["step"], 1)
                        dve.wait_ge(r["step"], k[0])
                    one(nc.vector.tensor_scalar(flat(sel), flat(key), t, None, ALU.is_gt, ALU.add, accum_out=cnt))
                    dve.wait_ge(r["sum"], VALUE_BITS + 2)
                    one(nc.vector.tensor_scalar(need, pc[:, 0:1], -1.0, float(CAP), ALU.mult, ALU.add))
                    one(nc.vector.tensor_scalar(flat(sel), flat(key), t, FAR, ALU.not_equal, ALU.mult))
                    one(nc.vector.tensor_tensor(flat(idx), flat(idx), flat(sel), ALU.add))
                    one(nc.vector.memset(bitf, float(1 << (INDEX_BITS - 1))))
                    one(nc.vector.memset(lim, 0.0))
                    with dve.Fori(1, INDEX_BITS + 1) as i:
                        n = [0]

                        def step(ins):
                            n[0] += 1
                            ins.then_inc(rt["step"], 1)
                            dve.wait_ge(rt["step"], i * STEPS + n[0])
                        step(nc.vector.tensor_tensor(cand, lim, bitf, ALU.add))
                        step(nc.vector.tensor_scalar(flat(sel), flat(idx), cand, None, ALU.is_lt, ALU.add, accum_out=cnt))
                        dve.wait_ge(r["tb"], i + 1)
                        step(nc.vector.tensor_tensor(tot, pc[:, 0:1], need, ALU.is_lt))
                        step(nc.vector.tensor_tensor(tot, tot, bitf, ALU.mult))
                        step(nc.vector.tensor_tensor(lim, lim, tot, ALU.add))
                        step(nc.vector.tensor_scalar(bitf, bitf, 0.5, None, ALU.mult))
                        while n[0] < STEPS:
                            n[0] += 1
                            dve.sem_inc(rt["step"], 1)
                    one(nc.vector.tensor_scalar(flat(sel), flat(key), t, None, ALU.is_gt))
                    one(nc.vector.scalar_tensor_tensor(flat(sel), flat(idx), lim, flat(sel), ALU.is_le, ALU.add))
                    one(nc.vector.tensor_tensor_scan(flat(key), flat(sel), flat(sel), 0.0, ALU.add, ALU.max))
                    one(nc.vector.tensor_copy(cnt, key[:, NB - 1, N - 1:N]))
            with nc.Block() as block:
                @block.tensor
                def _(pe):
                    nc.tensor.matmul(pc[:, 0:1], prefix, cnt, start=True, stop=True).then_inc(r["tc"], 1)

                @block.vector
                def _(dve):
                    dve.wait_ge(r["tc"], 2)
                    nc.vector.tensor_scalar(offs, pc[:, 0:1], 0.0, None, ALU.add)
            with nc.Block() as block:
                @block.vector
                def _(dve):
                    nc.vector.scalar_tensor_tensor(flat(key), flat(key), offs, flat(sel), ALU.add, ALU.mult)
            ru = Round(nc, "chu", ["turn", "copy"], 1)
            pos = sb("pos", [N, NT * E], I32)
            low = sb("low", [N, NT * E], I32)
            with nc.Block() as block:
                @block.tensor
                def _(pe):
                    for k in range(NB):
                        w = min(P, NT * E - k * P)
                        if k >= 2:
                            pe.wait_ge(ru["copy"], k)
                        nc.tensor.transpose(pk[k % 2][0:N, 0:w], key[0:w, k, :], c.ident[0:w, 0:w]).then_inc(ru["turn"], 1)

                @block.vector
                def _(dve):
                    for k in range(NB):
                        w = min(P, NT * E - k * P)
                        dve.wait_ge(ru["turn"], k + 2)
                        nc.vector.tensor_scalar(pos[:, k * P:k * P + w], pk[k % 2][0:N, 0:w], 1.0, None, ALU.subtract).then_inc(ru["copy"], 1)
                    dve.wait_ge(ru["copy"], NB + 1)
                    nc.vector.tensor_scalar(low[:, :], pos[:, :], LOW - 1, None, ALU.bitwise_and).then_inc(ru["copy"], 1)
                    dve.wait_ge(ru["copy"], NB + 2)
                    nc.vector.tensor_copy(lo_b[:, :, :].rearrange("b j e -> b (j e)"), low[:, :])
                    nc.vector.tensor_scalar(pos[:, :], pos[:, :], LOW.bit_length() - 1, None, ALU.arith_shift_right).then_inc(ru["copy"], 1)
                    dve.wait_ge(ru["copy"], NB + 3)
                    nc.vector.tensor_copy(hi_b[:, :, :].rearrange("b j e -> b (j e)"), pos[:, :])
            for x in (r, rs, rt, ru):
                x.close()
        with ExitStack() as ctx:
            sb = lambda n, s, d=F32: ctx.enter_context(nc.sbuf_tensor("cl_" + n, s, d))
            ps = lambda n, s: ctx.enter_context(nc.psum_tensor("cl_" + n, s, F32))
            irow, jrow, irow_b = sb("irow", [N, LOW]), sb("jrow", [N, NT]), sb("irow_b", [N, LOW], BF16)
            img = sb("img", [N, 1])
            one_h = sb("one_h", [N, 2, E, HIGH], BF16)
            A = sb("A", [N, 2, E, 2 * HIGH], BF16)
            B = sb("B", [N, 2, E, LOW], BF16)
            zero = sb("zero", [N, 512], BF16)
            lists = sb("lists", [2 * HIGH, E, LOW])
            HALFE = E * LOW // 512
            pl = [ps(f"pl{k}", [2 * HIGH, 512 // LOW, LOW]) for k in range(HALFE)]
            px = ps("px", [P, E, TILES])
            r = Round(nc, "cls", ["hot", "low", "A", "mm"], G)
            q = Round(nc, "clq", ["zero", "end", "copy", "idx", "f"], 1)
            PE_ = 512 // LOW
            with nc.Block() as block:
                @block.gpsimd
                def _(pool):
                    nc.gpsimd.iota(irow[:, :], [[1, LOW]], base=0, channel_multiplier=0, allow_small_or_imprecise_dtypes=True)
                    nc.gpsimd.iota(jrow[:, :], [[1, NT]], base=0, channel_multiplier=0, allow_small_or_imprecise_dtypes=True)
                    nc.gpsimd.iota(img[:, :], [[1, 1]], base=0, channel_multiplier=1, allow_small_or_imprecise_dtypes=True)
                    nc.gpsimd.memset(zero[:, :], 0.0)
            with nc.Block() as block:
                @block.vector
                def _(dve):
                    nc.vector.tensor_copy(irow_b[:, :], irow[:, :])
            with nc.Block() as block:
                @block.tensor
                def _(pe):
                    for k in range(HALFE):
                        last = nc.tensor.matmul(pl[k][:, :, :].rearrange("h e l -> h (e l)"), zero[:, 0:2 * HIGH], zero[:, :], start=True, stop=False,
                                                skip_group_check=True)
                    with pe.Fori(1, G + 1) as i:
                        for k in range(G):
                            s = k % 2
                            pe.wait_ge(r["A"], r.now(i, k))
                            pe.wait_ge(r["low"], r.now(i, k))
                            for e in range(E):
                                last = nc.tensor.matmul(pl[e // PE_][:, e % PE_, :], A[:, s, e, :], B[:, s, e, :], start=False, stop=False,
                                                        skip_group_check=True)
                            last.then_inc(r["mm"], 1)

                used = lambda i, k: r.now(i, k) - (1 if k == 0 else 2)
                column = lambda i, k: bass.ds(i * G + (k - G), 1)

                @block.scalar
                def _(act):
                    with act.Fori(1, G + 1) as i:
                        for k in range(G):
                            s = k % 2
                            act.wait_ge(r["mm"], used(i, k))
                            act.wait_ge(r["hot"], r.now(i, k))
                            apart(c, act)
                            nc.scalar.activation(A[:, s, :, 0:HIGH], one_h[:, s], ACT.Copy, scale=img[:, :])
                            nc.scalar.activation(A[:, s, :, HIGH:], one_h[:, s], ACT.Copy, scale=jrow[:, column(i, k)]).then_inc(r["A"], 1)

                @block.vector
                def _(dve):
                    with dve.Fori(1, G + 1) as i:
                        for k in range(G):
                            hi = hi_b[:, column(i, k), :].rearrange("b o e -> b (o e)")
                            dve.wait_ge(r["A"], used(i, k))
                            nc.vector.tensor_tensor(one_h[:, k % 2], across(irow_b[:, 0:HIGH], 1, E), across(hi, 2, HIGH), ALU.is_equal).then_inc(r["hot"], 1)
                            dve.wait_ge(r["mm"], used(i, k))
                            lo = lo_b[:, column(i, k), :].rearrange("b o e -> b (o e)")
                            nc.vector.tensor_tensor(B[:, k % 2], across(irow_b[:, :], 1, E), across(lo, 2, LOW), ALU.is_equal).then_inc(r["low"], 1)
            with nc.Block() as block:
                @block.scalar
                def _(act):
                    for k in range(HALFE):
                        last = nc.scalar.activation(lists[:, k * PE_:(k + 1) * PE_, :], pl[k][:, :, :], ACT.Copy)
                    last.then_inc(q["copy"], 1)

                @block.tensor
                def _(pe):
                    pe.wait_ge(q["copy"], 2)
                    for e in range(E):
                        for h in range(2):
                            last = nc.tensor.matmul(px[h * LOW:(h + 1) * LOW, e, :], lists[:, e, :], comb[:, h, :], start=True, stop=True)
                    last.then_inc(q["idx"], 1)

                @block.vector
                def _(dve):
                    dve.wait_ge(q["idx"], 2)
                    pad = across(con[:, 2 * P + 1:], 1, E)
                    nc.vector.tensor_tensor(slots[:, :].rearrange("p (e a) -> p e a", a=TILES), px[:, :, :], pad, ALU.add)
            r.close()
            q.close()


def run_experts(c, slots, E, F4, TILES, ROW):
    nc = c.nc
    BATCH = 4
    batches = [(a, min(BATCH, TILES - a)) for a in range(0, TILES, BATCH)]
    NBT = len(batches)
    table, acc = c.dram["table"], c.dram["acc"]
    ctx = ExitStack()
    with ctx:
        sb = lambda n, s, d=F32: ctx.enter_context(nc.sbuf_tensor("ex_" + n, s, d))
        ps = lambda n, s: ctx.enter_context(nc.psum_tensor("ex_" + n, s, F32))
        r = Round(nc, "exp", ["idx", "placed"], 1, dma=["bias", "w0", "w1", "v0", "v1"])
        gsem = [nc.alloc_semaphore(name=f"exp_gather{s}") for s in range(2)]
        ssem = nc.alloc_semaphore(name="exp_scatter")
        b = Round(nc, "exb", ["turned", "xt", "f2", "sum", "y"], NBT)
        f = Round(nc, "exf", ["f1", "gelu"], NBT * F4)
        w1, w2 = sb("w1", [P, 2, F4 * P]), sb("w2", [P, 2, F4, P])
        b2 = sb("b2", [P, E, P])
        ix = sb("ix", [P, 2, TILES], U32)
        g = sb("g", [P, 2, TILES, ROW])
        xt = sb("xt", [P, BATCH * P])
        hid = sb("hid", [P, F4, BATCH * P])
        y = sb("y", [P, TILES, P])
        pt = ps("pt", [P, BATCH * P])
        pf = [ps(f"pf{k}", [P, BATCH * P]) for k in range(2)]
        po = ps("po", [P, BATCH, P])
        with nc.Block() as block:
            @block.sync
            def _(sp):
                sp.dma_start(b2[:, :, :], c.dram["eb2b"]).then_inc(r["bias"], 16)
                sp.wait_ge(r["bias"], 32)

            @block.vector
            def _(dve):
                for e in (1, 2):
                    nc.vector.tensor_copy(ix[:, e % 2, :], slots[:, (e - 1) * TILES:e * TILES])
        with nc.Block() as block:
            GATHERED = 16 * TILES

            def pairs(eng, body):
                with eng.Fori(1, E, 2) as e:
                    body(e, 1)
                    body(e + 1, 0)

            @block.sync
            def _(sp):
                def load(e, s):
                    at = sp.snap(e - 1)
                    sp.wait_ge(b["f2"], e * NBT - NBT)
                    sp.dma_start(w1[:, s, :], c.dram["ew1"][:, bass.ds(at, 1), :].rearrange("p o h -> p (o h)")).then_inc(r[f"w{s}"], 16)
                    sp.dma_start(w2[:, s, :, :], c.dram["ew2"][:, bass.ds(at, 1), :, :].rearrange("p o k d -> p (o k) d")).then_inc(r[f"v{s}"], 16)
                for e in (1, 2):
                    s = e % 2
                    sp.dma_start(w1[:, s, :], c.dram["ew1"][:, e - 1, :]).then_inc(r[f"w{s}"], 16)
                    sp.dma_start(w2[:, s, :, :], c.dram["ew2"][:, e - 1, :, :]).then_inc(r[f"v{s}"], 16)
                with sp.Fori(3, E, 2) as e:
                    load(e, 1)
                    load(e + 1, 0)

            @block.gpsimd
            def _(pool):
                def gather(e, s):
                    for a in range(TILES):
                        nc.gpsimd.indirect_dma_start(out=g[:, s, a, :], out_offset=None, in_=table[:, :],
                                                     in_offset=bass.IndirectOffsetOnAxis(ap=ix[:, s, a:a + 1], axis=0)).then_inc(gsem[s], 16)

                def scatter(e, s):
                    for k, (a0, n) in enumerate(batches):
                        pool.wait_ge(b["y"], b.now(e, k))
                        apart(c, pool)
                        for a in range(a0, a0 + n):
                            nc.gpsimd.indirect_dma_start(out=acc[:, :], out_offset=bass.IndirectOffsetOnAxis(ap=ix[:, s, a:a + 1], axis=0),
                                                         in_=y[:, a, :], in_offset=None, compute_op=ALU.add).then_inc(ssem, 16)
                    pool.wait_ge(ssem, e * GATHERED)
                    pool.sem_inc(r["placed"], 1)
                gather(1, 1)
                with pool.Fori(1, E - 2, 2) as e:
                    pool.wait_ge(r["idx"], e)
                    apart(c, pool)
                    gather(e + 1, 0)
                    scatter(e, 1)
                    pool.wait_ge(r["idx"], e + 1)
                    apart(c, pool)
                    gather(e + 2, 1)
                    scatter(e + 1, 0)
                pool.wait_ge(r["idx"], E - 1)
                gather(E, 0)
                scatter(E - 1, 1)
                scatter(E, 0)

            @block.tensor
            def _(pe):
                def body(e, s):
                    pe.wait_ge(gsem[s], (e * 8 + (8 if s else 0)) * TILES)
                    pe.wait_ge(r[f"w{s}"], e * 8 + (24 if s else 16))
                    pe.wait_ge(r[f"v{s}"], e * 8 + (24 if s else 16))
                    for k, (a0, n) in enumerate(batches):
                        pe.wait_ge(b["xt"], b.now(e, k) - 1)
                        for a in range(n):
                            last = nc.tensor.transpose(pt[:, a * P:(a + 1) * P], g[:, s, a0 + a, 0:P], c.ident[:, :])
                        last.then_inc(b["turned"], 1)
                        pe.wait_ge(b["xt"], b.now(e, k))
                        for q in range(F4):
                            pe.wait_ge(f["gelu"], f.now(e, k * F4 + q) - 2)
                            nc.tensor.matmul(pf[q % 2][:, 0:n * P], w1[:, s, q * P:(q + 1) * P], xt[:, 0:n * P], start=True, stop=True).then_inc(f["f1"], 1)
                        pe.wait_ge(f["gelu"], f.now(e, k * F4 + F4 - 1))
                        pe.wait_ge(b["sum"], b.now(e, k) - 1)
                        for a in range(n):
                            for q in range(F4):
                                last = nc.tensor.matmul(po[:, a, :], hid[:, q, a * P:(a + 1) * P], w2[:, s, q, :], start=(q == 0), stop=(q == F4 - 1))
                        last.then_inc(b["f2"], 1)
                pairs(pe, body)

            @block.scalar
            def _(act):
                def body(e, s):
                    for k, (a0, n) in enumerate(batches):
                        act.wait_ge(b["turned"], b.now(e, k))
                        nc.scalar.activation(xt[:, 0:n * P], pt[:, 0:n * P], ACT.Copy).then_inc(b["xt"], 1)
                        act.wait_ge(b["f2"], b.now(e, k) - 1)
                        for q in range(F4):
                            act.wait_ge(f["f1"], f.now(e, k * F4 + q))
                            apart(c, act)
                            at = COLS["eb1"][0] + q
                            nc.scalar.activation(hid[:, q, 0:n * P], pf[q % 2][:, 0:n * P], ACT.Gelu_apprx_tanh,
                                                 bias=c.cols[:, bass.ds(e * F4 + (at - F4), 1)]).then_inc(f["gelu"], 1)
                pairs(act, body)

            @block.vector
            def _(dve):
                def body(e, s):
                    for k, (a0, n) in enumerate(batches):
                        dve.wait_ge(b["f2"], b.now(e, k))
                        if k == 0:
                            dve.wait_ge(r["placed"], e)
                        bias = b2[:, bass.ds(e - 1, 1), :].rearrange("p o d -> p (o d)")
                        nc.vector.tensor_tensor(y[:, a0:a0 + n, :], po[:, 0:n, :], across(bias, 1, n), ALU.add).then_inc(b["sum"], 1)
                        dve.wait_ge(b["sum"], b.now(e, k))
                        dve.wait_ge(gsem[s], (e * 8 + (8 if s else 0)) * TILES)
                        prob = g[:, s, a0:a0 + n, bass.ds(e + (P - 1), 1)].to_broadcast([P, n, P])
                        nc.vector.tensor_tensor(y[:, a0:a0 + n, :], y[:, a0:a0 + n, :], prob, ALU.mult).then_inc(b["y"], 1)
                with dve.Fori(1, E - 2, 2) as e:
                    for s, d in ((1, 0), (0, 1)):
                        body(e + d, s)
                        dve.wait_ge(r["placed"], e + (d + 1))
                        nc.vector.tensor_copy(ix[:, s, :], slots[:, bass.ds((e + (d + 1)) * TILES, TILES)]).then_inc(r["idx"], 1)
                body(E - 1, 1)
                body(E, 0)
        b.close()
        f.close()
        r.close()
        nc.clear_and_free_semaphores([*gsem, ssem])
        nc.all_engine_barrier()


def last_norm(c, arow, out):
    nc, NT, N, G = c.nc, c.NT, c.N, c.G
    ctx = ExitStack()
    with ctx:
        sb = lambda n, s, d=F32: ctx.enter_context(nc.sbuf_tensor("ln_" + n, s, d))
        r = Round(nc, "lns", ["stat", "aggr", "nm", "ln", "rstd", "y"], 1, dma=["in0", "in1", "out"])
        x = sb("x", [N, 2, G, P])
        y = sb("y", [N, G, P])
        st, mv, rstd = sb("st", [N, G, 6]), sb("mv", [N, G, 2]), sb("rstd", [N, G])
        with nc.Block() as block:
            @block.sync
            def _(sp):
                for i in range(G):
                    if i >= 2:
                        sp.wait_ge(r["y"], i)
                    sp.dma_start(x[:, i % 2], arow[:, i * G:(i + 1) * G, :]).then_inc(r[f"in{i % 2}"], 16)

            @block.scalar
            def _(act):
                nc.scalar.preload_act_table_set(LN_SETS)
                for i in range(G):
                    act.wait_ge(r["aggr"], i + 2)
                    if i:
                        act.wait_ge(r["y"], i + 1)
                    nc.scalar.activation(rstd[:, :], mv[:, :, 1], ACT.Ln, bias=c.eps[0:N, 0:1]).then_inc(r["ln"], 1)
                    act.wait_ge(r["ln"], i + 2)
                    nc.scalar.activation(rstd[:, :], rstd[:, :], ACT.Exp, scale=-0.5).then_inc(r["rstd"], 1)
                    act.wait_ge(r["y"], i + 2)
                    act.dma_start(out[:, i * G:(i + 1) * G, :], y[:, :, :]).then_inc(r["out"], 16)
                act.wait_ge(r["out"], 16 * G + 16)

            @block.vector
            def _(dve):
                for i in range(G):
                    dve.wait_ge(r[f"in{i % 2}"], 32 + 16 * (i // 2))
                    for k in range(G):
                        last = nc.vector.bn_stats(st[:, k, :], x[:, i % 2, k, :])
                    last.then_inc(r["stat"], 1)
                    dve.wait_ge(r["stat"], i + 2)
                    for k in range(G):
                        last = nc.vector.bn_aggr(mv[:, k, :], st[:, k, :])
                    last.then_inc(r["aggr"], 1)
                    dve.wait_ge(r["rstd"], i + 2)
                    if i:
                        dve.wait_ge(r["out"], 16 + 16 * i)
                    for k in range(G):
                        last = nc.vector.tensor_scalar(y[:, k, :], x[:, i % 2, k, :], mv[:, k, 0:1], rstd[:, k:k + 1], ALU.subtract, ALU.mult)
                    last.then_inc(r["y"], 1)
        r.close()


def head_masks(c, tag, qmask, scale, clear):
    nc = c.nc
    r = Round(nc, tag + "msk", ["sum"], 1)
    with nc.Block() as block:
        @block.vector
        def _(dve):
            for x in range(2):
                half = c.ident[:, :].rearrange("p (j x d) -> p x j d", x=2, d=16)[:, x]
                last = nc.vector.tensor_reduce(qmask[:, x:x + 1], half, AX.XY, ALU.add)
            last.then_inc(r["sum"], 1)
            dve.wait_ge(r["sum"], 2)
            nc.vector.tensor_scalar(qmask[:, :], qmask[:, :], scale, None, ALU.mult)

        @block.gpsimd
        def _(pool):
            for t in clear:
                nc.gpsimd.memset(t[:, :, :], 0.0)
    r.close()


def apart(c, eng):
    eng.sem_inc(c.passed, 1)


def old(eng, sem, value):
    there = not isinstance(value, int) or value > 0
    if there and eng is not None:
        eng.wait_ge(sem, value)
    return there


def tower(nc, dram, out, images):
    with ExitStack() as ctx:
        c = Core(nc, ctx, dram, images)
        c.mo_dram = dram["mo"]
        constants(c)
        with ExitStack() as early:
            c.gw = early.enter_context(nc.sbuf_tensor("gw", [P, c.NT], F32))
            c.bw = early.enter_context(nc.sbuf_tensor("bw", [P, c.NT], F32))
            c.rstd = early.enter_context(nc.sbuf_tensor("rstd", [P, images], F32))
            c.nmr = early.enter_context(nc.sbuf_tensor("nmr", [P, images], F32))
            tokens_stage(c)
            mamba_stage(c)
        attention_stage(c)
        top_attention_stage(c)
        relu_attention_stage(c)
        experts_stage(c, out)


def dump(c, out):
    nc = c.nc
    r = Round(nc, "out", [], 1, dma=["out"])
    with nc.Block() as block:
        @block.sync
        def _(sp):
            sp.dma_start(out, c.H[:, :]).then_inc(r["out"], 16)
            sp.wait_ge(r["out"], 32)
    r.close()


def layout(inputs):
    import numpy as np
    f = {k: np.asarray(v) for k, v in inputs.items()}
    a, b = "L0_attn_", "L0_ffn_"
    d = {}
    x = f["x"]
    N, C, S, _ = x.shape
    G = S // PATCH
    rows = lambda y, g: y.reshape(N, C, g, PATCH, g, PATCH).transpose(1, 3, 5, 0, 2, 4).reshape(P, N, g * g)
    d["xbase"] = rows(x, G)
    d["xoff"] = rows(np.pad(x, ((0, 0), (0, 0), (HP, HP), (HP, HP))), G + 1)
    pix = lambda y: y.reshape(5, 2, G, PATCH, G, PATCH).transpose(1, 3, 5, 0, 2, 4).reshape(P, 5, G * G)
    d["gamma"], d["beta"] = pix(f["L0_tok_gamma"]), pix(f["L0_tok_beta"])
    d["tokW"] = f["L0_tok_W"].reshape(P, 5, P).transpose(2, 1, 0)
    halves = lambda w: w.reshape(-1, P, w.shape[1]).transpose(1, 0, 2)
    d["w_in"] = f[a + "in_proj_w"]
    d["taps"] = np.broadcast_to(f[a + "conv_w"].T, (P, 4, 256))
    d["w_x"] = halves(f[a + "x_proj_w"])
    d["w_dt"] = halves(f[a + "dt_proj_w"])
    d["w_out"] = halves(f[a + "out_proj_w"])
    d["A_log"] = np.broadcast_to(f[a + "A_log"], (P, 16))
    for n, k in (("wq", "wq_w"), ("wk", "wk_w"), ("wv", "wv_w"), ("wo", "wo_w"), ("w1", "ffn_w1")):
        d[n] = f[a + k]
    d["w2"] = halves(f[a + "ffn_w2"])
    d["wg"] = halves(f[a + "gate_w"])
    d["qkv"] = f[b + "qkv_w"].T
    d["wo2"] = f[b + "wo_w"].T
    for n in "qkvo":
        d["w3" + n] = f["L1_attn_W" + n]
    d["bv3"] = np.broadcast_to(f["L1_attn_bv"], (P, P))
    m = "L1_ffn_"
    d["wgate"] = f[m + "gate_w"]
    d["ew1"] = f[m + "w1"].transpose(1, 0, 2)
    d["ew2"] = f[m + "w2"].reshape(16, 4, P, P).transpose(2, 0, 1, 3)
    d["sw1"] = f[m + "sw1"]
    d["sw2"] = halves(f[m + "sw2"])
    vec = {"tok_b": "L0_tok_b", "conv_b": a + "conv_b", "dt_b": a + "dt_proj_b", "D": a + "D", "n1g": a + "norm1_g",
           "n1b": a + "norm1_b", "n2g": a + "norm2_g", "n2b": a + "norm2_b", "n3g": a + "norm3_g", "n3b": a + "norm3_b",
           "ang": a + "attn_ln_g", "anb": a + "attn_ln_b", "wq_b": a + "wq_b", "wk_b": a + "wk_b", "wv_b": a + "wv_b",
           "wo_b": a + "wo_b", "gate_b": a + "gate_b", "f_b1": a + "ffn_b1", "f_b2": a + "ffn_b2", "pos_b": b + "pos_b",
           "o2_b": b + "wo_b", "q3_b": "L1_attn_bq", "k3_b": "L1_attn_bk", "v3_b": "L1_attn_bv", "o3_b": "L1_attn_bo",
           "g3": "L1_attn_gamma", "b3": "L1_attn_beta", "sb1": m + "sb1", "sb2": m + "sb2"}
    cols = np.zeros((P, COLS_WIDTH), np.float32)
    def put(n, v):
        at, w = COLS[n]
        cols[:, at:at + w] = v.reshape(w, P).T
    for n, k in vec.items():
        put(n, f[k])
    put("pos_w", f[b + "pos_w"].reshape(P, 3).T)
    for k, n in enumerate(("q2_b", "k2_b", "v2_b")):
        put(n, f[b + "qkv_b"][k * P:(k + 1) * P])
    put("eb1", f[m + "b1"])
    put("eb2", f[m + "b2"])
    d["cols"] = cols
    d["sb2b"] = np.broadcast_to(f[m + "sb2"], (P, P))
    d["eb2b"] = np.broadcast_to(f[m + "b2"], (P, 16, P))
    E, NT = 16, G * G
    T = N * NT
    cap = expert_capacity(T, E)
    tiles = -(-cap // P)
    p = np.arange(P)
    same = p[:, None] % E == p[None, :] % E
    slot = np.arange(tiles)[None, :] * P + p[:, None]
    pad = np.where(slot >= cap, T + slot - cap, 0)
    d["con"] = np.concatenate([same, same & (p[:, None] < p[None, :]), (p // E)[:, None], pad], 1).astype(np.float32)
    comb = np.zeros((4 * tiles, 2, tiles), np.float32)
    for a in range(tiles):
        for h in range(2):
            comb[2 * a + h, h, a] = NT
            comb[2 * tiles + 2 * a + h, h, a] = 1.0
    d["comb"] = comb
    return {k: np.ascontiguousarray(v) for k, v in d.items()}, N


def program(nc, arrays, out_shape, images):
    dram = {n: nc.dram_tensor(f"in_{n}", a.shape, mybir.dt.from_np(a.dtype), kind="ExternalInput").ap() for n, a in arrays.items()}
    T = images * 169
    for n, w in (("table", P + 16), ("acc", P)):
        dram[n] = nc.dram_tensor(f"moe_{n}", [T + P, w], F32, kind="Internal").ap()
    dram["mo"] = nc.dram_tensor("mamba_out", [P, T], F32, kind="Internal").ap()
    out = nc.dram_tensor("out", out_shape, F32, kind="ExternalOutput").ap()
    tower(nc, dram, out, images)


def kernel(**inputs):
    import numpy as np
    import concourse.bacc as bacc
    from concourse.bass_utils import run_bass_kernel_spmd
    arrays, images = layout(inputs)
    nc = bacc.Bacc("TRN2", target_bir_lowering=False, num_devices=1)
    program(nc, arrays, [images, 169, P], images)
    return run_bass_kernel_spmd(nc, [{f"in_{k}": v for k, v in arrays.items()}], core_ids=[0]).results[0]["out"]
```
